# Optimizing a Trainium2 kernel written in Bass

```python
import numpy as np
import jax
import jax.numpy as jnp

def _softmax(x, axis=-1):
    return jax.nn.softmax(x, axis=axis)

def _gelu(x):
    return jax.nn.gelu(x, approximate=True)

def _silu(x):
    return jax.nn.silu(x)

def _sigmoid(x):
    return jax.nn.sigmoid(x)

def _layernorm(x, axis=-1, eps=1e-05):
    m = jnp.mean(x, axis=axis, keepdims=True)
    v = jnp.var(x, axis=axis, keepdims=True)
    return (x - m) / jnp.sqrt(v + eps)

def _scatter_add(tgt, idx, src, axis=0):
    return tgt.at[idx].add(src)

def _segment_sum(src, seg, n):
    return jax.ops.segment_sum(src, seg, n)
kernel_name = 'mk_gps_d1_gnn_r8_006745'

def setup_inputs(seed: int=0):
    np.random.seed(seed)
    _w = jnp.asarray

    def _rec_inputs():
        import jax
        import jax.numpy as jnp
        _gk = jax.random.key(seed)
        x = -0.0003713 + 1 * jax.random.normal(jax.random.fold_in(_gk, 1), (6250, 256), jnp.float32)
        _s = jax.random.randint(jax.random.fold_in(_gk, 2), (100000,), 0, 6250, jnp.int32)
        _d = jax.random.randint(jax.random.fold_in(_gk, 3), (100000,), 0, 6250, jnp.int32)
        _loop = jnp.arange(6250, dtype=jnp.int32)
        src = jnp.concatenate([_s, _d, _loop])
        dst = jnp.concatenate([_d, _s, _loop])
        _o = jnp.argsort(dst, stable=True)
        src = src[_o]
        dst = dst[_o]
        edge_weight = jax.random.uniform(jax.random.fold_in(_gk, 12), (206250,), jnp.float32, 0.0, 0.999999)
        return (x, src, dst, edge_weight)
    x, src, dst, edge_weight = _rec_inputs()

    def _L0_gnn_setup():
        import jax, jax.numpy as jnp
        import numpy as np
        N_NODES = 6250
        N_EDGES = 200000
        F_IN = 256
        F_OUT = 256

        def _gcn_conv(x, src, dst, ew, W, b, n_nodes):
            xW = x @ W
            deg = jax.ops.segment_sum(ew, dst, num_segments=n_nodes) + 1.0
            dinv = jnp.where(deg > 0, jax.lax.rsqrt(deg), 0.0)
            norm = dinv[src] * ew * dinv[dst]
            agg = jax.ops.segment_sum(norm[:, None] * xW[src], dst, num_segments=n_nodes)
            agg = agg + (dinv * dinv)[:, None] * xW
            return agg + b
        key = jax.random.key(seed)
        ks = jax.random.split(key, 7)
        x = jax.random.normal(ks[0], (N_NODES, F_IN), dtype=jnp.float32)
        edge_index = jax.random.randint(ks[1], (2, N_EDGES), 0, N_NODES, dtype=jnp.int64)
        edge_weight = jax.random.uniform(ks[2], (N_EDGES,), dtype=jnp.float32)
        W1 = jax.random.normal(ks[3], (F_IN, F_OUT), dtype=jnp.float32) * (1.0 / np.sqrt(F_IN))
        b1 = jnp.zeros((F_OUT,), dtype=jnp.float32)
        W2 = jax.random.normal(ks[4], (F_OUT, F_OUT), dtype=jnp.float32) * (1.0 / np.sqrt(F_OUT))
        b2 = jnp.zeros((F_OUT,), dtype=jnp.float32)
        return {'x': x, 'edge_index': edge_index, 'edge_weight': edge_weight, 'W1': W1, 'b1': b1, 'W2': W2, 'b2': b2}
    _L0_gnn_all = _L0_gnn_setup()
    _L0_gnn_in = {k: v for k, v in _L0_gnn_all.items() if k in ('W1', 'b1', 'W2', 'b2')}
    del _L0_gnn_all

    def _L0_mix_setup():
        import jax, jax.numpy as jnp
        import numpy as np
        D_MODEL = 256
        NUM_HEADS = 8
        DEPTH = D_MODEL // NUM_HEADS
        B, L = (32, 512)

        def _feature_map(x):
            return jax.nn.elu(x) + 1.0
        key = jax.random.key(seed)
        ks = jax.random.split(key, 9)
        sc = 1.0 / np.sqrt(D_MODEL)
        return {'x': jax.random.normal(ks[0], (B, L, D_MODEL), dtype=jnp.float32), 'wq': jax.random.normal(ks[1], (D_MODEL, D_MODEL), dtype=jnp.float32) * sc, 'bq': jnp.zeros((D_MODEL,), dtype=jnp.float32), 'wk': jax.random.normal(ks[2], (D_MODEL, D_MODEL), dtype=jnp.float32) * sc, 'bk': jnp.zeros((D_MODEL,), dtype=jnp.float32), 'wv': jax.random.normal(ks[3], (D_MODEL, D_MODEL), dtype=jnp.float32) * sc, 'bv': jnp.zeros((D_MODEL,), dtype=jnp.float32), 'wo': jax.random.normal(ks[4], (D_MODEL, D_MODEL), dtype=jnp.float32) * sc, 'bo': jnp.zeros((D_MODEL,), dtype=jnp.float32)}
    _L0_mix_all = _L0_mix_setup()
    _L0_mix_in = {k: v for k, v in _L0_mix_all.items() if k in ('wq', 'bq', 'wk', 'bk', 'wv', 'bv', 'wo', 'bo')}
    del _L0_mix_all

    def _L0_ffn_setup():
        import jax, jax.numpy as jnp
        import numpy as np
        E = 8
        K = 2
        D = 256
        H = 512
        DOUT = 256
        EPS = 1e-05
        key = jax.random.key(seed)
        ks = jax.random.split(key, 9)
        s = 0.02
        return {'x': jax.random.normal(ks[0], (4, 1024, D), jnp.float32), 'gamma': 1.0 + 0.05 * jax.random.normal(ks[1], (D,), jnp.float32), 'beta': 0.05 * jax.random.normal(ks[2], (D,), jnp.float32), 'Wr': 0.01 * jax.random.normal(ks[3], (D, E), jnp.float32), 'br': jnp.zeros((E,), jnp.float32), 'W1': s * jax.random.normal(ks[4], (E, D, H), jnp.float32), 'b1': s * jax.random.normal(ks[5], (E, H), jnp.float32), 'W2': s * jax.random.normal(ks[6], (E, H, DOUT), jnp.float32), 'b2': s * jax.random.normal(ks[7], (E, DOUT), jnp.float32)}
    _L0_ffn_all = _L0_ffn_setup()
    _L0_ffn_in = {k: v for k, v in _L0_ffn_all.items() if k in ('gamma', 'beta', 'Wr', 'br', 'W1', 'b1', 'W2', 'b2')}
    del _L0_ffn_all
    return {'x': x, 'src': src, 'dst': dst, 'edge_weight': edge_weight, 'L0_gnn_W1': _L0_gnn_in['W1'], 'L0_gnn_b1': _L0_gnn_in['b1'], 'L0_gnn_W2': _L0_gnn_in['W2'], 'L0_gnn_b2': _L0_gnn_in['b2'], 'L0_mix_wq': _L0_mix_in['wq'], 'L0_mix_bq': _L0_mix_in['bq'], 'L0_mix_wk': _L0_mix_in['wk'], 'L0_mix_bk': _L0_mix_in['bk'], 'L0_mix_wv': _L0_mix_in['wv'], 'L0_mix_bv': _L0_mix_in['bv'], 'L0_mix_wo': _L0_mix_in['wo'], 'L0_mix_bo': _L0_mix_in['bo'], 'L0_ffn_gamma': _L0_ffn_in['gamma'], 'L0_ffn_beta': _L0_ffn_in['beta'], 'L0_ffn_Wr': _L0_ffn_in['Wr'], 'L0_ffn_br': _L0_ffn_in['br'], 'L0_ffn_W1': _L0_ffn_in['W1'], 'L0_ffn_b1': _L0_ffn_in['b1'], 'L0_ffn_W2': _L0_ffn_in['W2'], 'L0_ffn_b2': _L0_ffn_in['b2']}

def reference(x, src, dst, edge_weight, L0_gnn_W1, L0_gnn_b1, L0_gnn_W2, L0_gnn_b2, L0_mix_wq, L0_mix_bq, L0_mix_wk, L0_mix_bk, L0_mix_wv, L0_mix_bv, L0_mix_wo, L0_mix_bo, L0_ffn_gamma, L0_ffn_beta, L0_ffn_Wr, L0_ffn_br, L0_ffn_W1, L0_ffn_b1, L0_ffn_W2, L0_ffn_b2):
    import jax
    import jax.numpy as jnp

    def _L0_gnn_ref(x, edge_index, edge_weight, W1, b1, W2, b2):
        import jax, jax.numpy as jnp
        import numpy as np
        N_NODES = 6250
        N_EDGES = 200000
        F_IN = 256
        F_OUT = 256

        def _gcn_conv(x, src, dst, ew, W, b, n_nodes):
            xW = x @ W
            deg = jax.ops.segment_sum(ew, dst, num_segments=n_nodes) + 1.0
            dinv = jnp.where(deg > 0, jax.lax.rsqrt(deg), 0.0)
            norm = dinv[src] * ew * dinv[dst]
            agg = jax.ops.segment_sum(norm[:, None] * xW[src], dst, num_segments=n_nodes)
            agg = agg + (dinv * dinv)[:, None] * xW
            return agg + b
        src = edge_index[0]
        dst = edge_index[1]
        n = x.shape[0]
        h1 = jax.nn.relu(_gcn_conv(x, src, dst, edge_weight, W1, b1, n))
        h2 = jax.nn.relu(_gcn_conv(h1, src, dst, edge_weight, W2, b2, n))
        return h2

    def _L0_mix_ref(x, wq, bq, wk, bk, wv, bv, wo, bo):
        import jax, jax.numpy as jnp
        import numpy as np
        D_MODEL = 256
        NUM_HEADS = 8
        DEPTH = D_MODEL // NUM_HEADS
        B, L = (32, 512)

        def _feature_map(x):
            return jax.nn.elu(x) + 1.0
        b, l, _ = x.shape
        q = (x @ wq + bq).reshape(b, l, NUM_HEADS, DEPTH)
        k = (x @ wk + bk).reshape(b, l, NUM_HEADS, DEPTH)
        v = (x @ wv + bv).reshape(b, l, NUM_HEADS, DEPTH)
        q = _feature_map(q)
        k = _feature_map(k)
        kv = jnp.einsum('blhd,blhe->bhde', k, v)
        k_sum = jnp.sum(k, axis=1)
        qkv = jnp.einsum('blhd,bhde->blhe', q, kv)
        normalizer = jnp.einsum('blhd,bhd->blh', q, k_sum) + 1e-06
        out = qkv / normalizer[..., None]
        out = out.reshape(b, l, D_MODEL)
        return out @ wo + bo

    def _L0_ffn_ref(x, gamma, beta, Wr, br, W1, b1, W2, b2):
        import jax, jax.numpy as jnp
        import numpy as np
        E = 8
        K = 2
        D = 256
        H = 512
        DOUT = 256
        EPS = 1e-05
        mu = jnp.mean(x, axis=-1, keepdims=True)
        var = jnp.mean(jnp.square(x - mu), axis=-1, keepdims=True)
        xn = (x - mu) * jax.lax.rsqrt(var + EPS) * gamma + beta
        logits = jnp.einsum('bsd,de->bse', xn, Wr) + br
        top_vals, top_idx = jax.lax.top_k(logits, K)
        w = jax.nn.softmax(top_vals, axis=-1)
        w_full = jnp.einsum('bsk,bske->bse', w, jax.nn.one_hot(top_idx, E, dtype=w.dtype))
        y = jnp.zeros(x.shape[:-1] + (DOUT,), x.dtype)
        for e in range(E):
            h = jax.nn.gelu(jnp.einsum('bsd,dh->bsh', xn, W1[e]) + b1[e], approximate=False)
            y_e = jnp.einsum('bsh,hd->bsd', h, W2[e]) + b2[e]
            y = y + y_e * w_full[..., e, None]
        return y
    edge_index = jnp.stack([src, dst])
    xn = _layernorm(x, axis=-1)
    x = x + _L0_gnn_ref(xn, edge_index, edge_weight, L0_gnn_W1, L0_gnn_b1, L0_gnn_W2, L0_gnn_b2) + _L0_mix_ref(xn[None], L0_mix_wq, L0_mix_bq, L0_mix_wk, L0_mix_bk, L0_mix_wv, L0_mix_bv, L0_mix_wo, L0_mix_bo)[0]
    x = x + _L0_ffn_ref(_layernorm(x, axis=-1)[None], L0_ffn_gamma, L0_ffn_beta, L0_ffn_Wr, L0_ffn_br, L0_ffn_W1, L0_ffn_b1, L0_ffn_W2, L0_ffn_b2)[0]
    return x

_drawn_inputs = setup_inputs


def setup_inputs(seed=0):
    import zlib

    import numpy as np

    out = dict(_drawn_inputs(seed))
    spreads = {'L0_gnn_b1': (0.0, 0.1),
     'L0_gnn_b2': (0.0, 0.1),
     'L0_mix_bq': (0.0, 2.0),
     'L0_mix_bk': (0.0, 2.0),
     'L0_mix_bv': (0.0, 0.1),
     'L0_mix_bo': (0.0, 0.1),
     'L0_ffn_br': (0.0, 0.1)}
    factors = {'edge_weight': 4.064,
     'L0_mix_wq': 8.0,
     'L0_mix_wk': 5.871,
     'L0_mix_wv': 3.731,
     'L0_ffn_gamma': 6.264,
     'L0_ffn_beta': 5.084,
     'L0_ffn_b1': 8.0,
     'L0_ffn_b2': 4.347}
    for name, (base, spread) in spreads.items():
        noise = np.random.default_rng([zlib.crc32(name.encode()), seed]).standard_normal(out[name].shape)
        drawn = base * np.exp(spread * noise) if base else spread * noise
        out[name] = jnp.asarray(drawn.astype(out[name].dtype))
    for name, factor in factors.items():
        out[name] = (out[name] * factor).astype(out[name].dtype)
    return out
```

```python
import concourse.bass as bass
from concourse import mybir
from contextlib import ExitStack

P = 128
F32 = mybir.dt.float32
BF16 = mybir.dt.bfloat16
I32 = mybir.dt.int32
U32 = mybir.dt.uint32
ALU = mybir.AluOpType
ACT = mybir.ActivationFunctionType
AX_X = mybir.AxisListType.X

N = 6250
D = 256
E = 206250
KH = D // P
NT = -(-N // P)
LAST = N - (NT - 1) * P
NP = 6336
WIN = 64
EDGE_TILES = 11
ROWS = -(-E // P)
GROUPS = -(-ROWS // EDGE_TILES)
ET = GROUPS * EDGE_TILES
EBLK = -(-ET // P)
GI = 6
CH = 256
ITERS = GROUPS // GI
G_REST = GROUPS - ITERS * GI
CHUNKS = -(-N // CH)
PRE_STEP = 1
RING = 3
SLOW_WIN = -(-N // WIN) + 0
NE, H = 8, 512
HC = H // P
HEADS, DEPTH = 8, 32
EPS = 1e-5
GATHER_INC = 16 * EDGE_TILES


def ge(eng, sem, value):
    if isinstance(value, int) and value <= 0:
        return
    eng.wait_ge(sem, value)


def gps_layer(nc, A, out):
    ctx = ExitStack()
    with ctx:
        def sb(name, shape, dt=F32):
            return ctx.enter_context(nc.sbuf_tensor(name, shape, dt))

        def sem(name):
            return ctx.enter_context(nc.semaphore(name))

        z_dram = [nc.dram_tensor(f"z{i}_rows", [N, D], F32).ap() for i in (1, 2)]
        res_dram = nc.dram_tensor("residual_rows", [N, D], F32).ap()
        stray_dram = nc.dram_tensor("stray_dst", [P, ET], F32).ap()

        big = sb("big", [P, 16384])
        aggT = sb("aggT", [P, KH, NP])
        srcT = sb("srcT", [P, ET], U32)
        dstL = sb("dstL", [P, ET])
        ewT = sb("ewT", [P, ET])
        rows = sb("rows", [P, RING, EDGE_TILES, D])
        S = sb("S", [P, 2, EDGE_TILES, WIN])
        idx = sb("idx", [P, RING, EDGE_TILES], U32)
        base_i = sb("base_i", [1, GROUPS], I32)
        flag_i = sb("flag_i", [1, 1], I32)
        ident = sb("ident", [P, P])
        ones = sb("ones", [P, P])
        iota_w = sb("iota_w", [P, WIN])
        win_start = sb("win_start", [P, SLOW_WIN])
        before = sb("before", [P, NE, NE])
        dinv = sb("dinv", [P, NT])
        stray_t = sb("stray_t", [P, EDGE_TILES])
        ps = ctx.enter_context(nc.psum_tensor("ps", [P, 8, 512], F32))

        scratch = sb("scratch", [P, 14, 512])
        small = sb("small", [P, 256])

        def piece(n, k=1):
            return scratch[:, n:n + k, :].rearrange("p a b -> p (a b)")

        def halves(v):
            return v.rearrange("p (k n) -> p k n", k=2)

        def rsqrt(dve, y, x, t):
            v = nc.vector
            v.tensor_scalar(t.bitcast(I32), x.bitcast(I32), 1, None, ALU.logical_shift_right)
            dve.drain()
            v.tensor_scalar(y.bitcast(I32), t.bitcast(I32), -1.0, float(0x5F3759DF), ALU.mult, ALU.add)
            dve.drain()
            for _ in range(3):
                v.tensor_tensor(t, y, y, ALU.mult)
                dve.drain()
                v.scalar_tensor_tensor(t, t, -0.5, x, ALU.mult, ALU.mult)
                dve.drain()
                v.scalar_tensor_tensor(y, t, 1.5, y, ALU.add, ALU.mult)
                dve.drain()

        o = EBLK * P
        row_dst_i = big[:, 0:o].bitcast(I32)
        row_src_i = big[:, o:2 * o].bitcast(I32)
        row_ew = big[:, 2 * o:3 * o]
        row_dst = big[:, 3 * o:4 * o]
        row_src = big[:, 4 * o:5 * o]
        dstT = big[:, 5 * o:5 * o + ET]
        stray = big[:, 6 * o:6 * o + ET]
        tmp_e = big[:, 7 * o:7 * o + ET]
        r0 = 8 * o
        frontier = big[:, r0:r0 + GROUPS]
        tmp_i = big[:, r0 + 256:r0 + 512].bitcast(I32)
        ew3 = rows[:, 0, :, :].rearrange("p a b -> p (a b)").bitcast(BF16)[:, 0:3 * ET]\
            .rearrange("p (t c) -> p t c", c=3)
        deg_oh = rows[:, 1, :, :].rearrange("p a b -> p (a b)").bitcast(BF16)[:, 0:3 * EDGE_TILES * WIN]\
            .rearrange("p (s t w) -> p s t w", s=3, w=WIN)
        FULL_BLK = EBLK - 1
        tail_row0 = FULL_BLK * P
        tail_rows = E // P - tail_row0
        tail_edges = E - (E // P) * P

        s_c = sem("const_step")
        s_pad = sem("pads_written")
        s_load = sem("edges_loaded")
        s_cast = sem("rows_cast")
        s_tr = sem("rows_transposed")
        s_ev = sem("edges_evacuated")
        s_base = sem("bases_spread")
        s_flag = sem("stray_count")
        s_flag2 = sem("stray_sum")
        s_stray = sem("strays_ready")
        s_sstore = sem("strays_stored")

        with nc.Block() as block:
            @block.sync
            def _(sp):
                for dst, src in ((row_dst_i, A["dst"]), (row_src_i, A["src"]), (row_ew, A["edge_weight"])):
                    sp.dma_start(dst[:, 0:FULL_BLK * P].rearrange("p (b c) -> p b c", c=P),
                                 src[0:FULL_BLK * P * P].rearrange("(b r c) -> r b c", r=P, c=P))\
                      .then_inc(s_load, 16)
                sp.wait_ge(s_pad, 3)
                for dst, src in ((row_dst_i, A["dst"]), (row_src_i, A["src"]), (row_ew, A["edge_weight"])):
                    e0 = tail_row0 * P
                    sp.dma_start(dst[0:tail_rows, FULL_BLK * P:EBLK * P],
                                 src[e0:e0 + tail_rows * P].rearrange("(r c) -> r c", c=P)).then_inc(s_load, 16)
                    sp.dma_start(dst[tail_rows:tail_rows + 1, FULL_BLK * P:FULL_BLK * P + tail_edges],
                                 src[e0 + tail_rows * P:E].rearrange("(r c) -> r c", r=1)).then_inc(s_load, 16)
                sp.wait_ge(s_stray, 1)
                sp.dma_start(stray_dram[:, :], dstT).then_inc(s_sstore, 16)
                sp.wait_ge(s_sstore, 16)

            @block.gpsimd
            def _(pool):
                g = nc.gpsimd
                g.memset(row_dst_i[:, FULL_BLK * P:EBLK * P], N).then_inc(s_pad, 1)
                g.memset(row_src_i[:, FULL_BLK * P:EBLK * P], 0).then_inc(s_pad, 1)
                g.memset(row_ew[:, FULL_BLK * P:EBLK * P], 0.0).then_inc(s_pad, 1)
                g.memset(ident[:, :], 0.0).then_inc(s_c, 1)
                g.memset(ones[:, :], 1.0).then_inc(s_c, 1)
                pool.wait_ge(s_c, 2)
                g.affine_select(out=ident[:, :], in_=ident[:, :], compare_op=ALU.not_equal, fill=1.0,
                                base=0, pattern=[[-1, P]], channel_multiplier=1).then_inc(s_c, 1)
                g.memset(frontier[:, 0:PRE_STEP + 1], 0.0).then_inc(s_c, 1)
                g.iota(tmp_i[:, 0:25 * GI], [[CH, 25], [0, GI]], base=0, channel_multiplier=0).then_inc(s_c, 1)
                pool.wait_ge(s_c, 5)
                g.tensor_copy(frontier[:, PRE_STEP + 1:GROUPS], tmp_i[:, 0:GROUPS - PRE_STEP - 1]).then_inc(s_c, 1)
                pool.wait_ge(s_c, 6)
                g.iota(tmp_i[:, 0:WIN], [[1, WIN]], base=0, channel_multiplier=0).then_inc(s_c, 1)
                pool.wait_ge(s_c, 7)
                g.tensor_copy(iota_w[:, :], tmp_i[:, 0:WIN]).then_inc(s_c, 1)
                pool.wait_ge(s_c, 8)
                g.iota(tmp_i[:, 0:SLOW_WIN], [[WIN, SLOW_WIN]], base=0, channel_multiplier=0).then_inc(s_c, 1)
                pool.wait_ge(s_c, 9)
                g.tensor_copy(win_start[:, :], tmp_i[:, 0:SLOW_WIN]).then_inc(s_c, 1)
                pool.wait_ge(s_c, 10)
                g.iota(tmp_i[:, 0:NE * NE], [[-1, NE], [1, NE]], base=0, channel_multiplier=0).then_inc(s_c, 1)
                pool.wait_ge(s_c, 11)
                g.tensor_copy(before[:, :, :].rearrange("p a b -> p (a b)"), tmp_i[:, 0:NE * NE]).then_inc(s_c, 1)

            @block.tensor
            def _(pe):
                pe.wait_ge(s_c, 3)
                for n, rows_f in enumerate((row_dst, row_ew, row_src)):
                    bank = 4 * (n % 2)
                    pe.wait_ge(s_cast, n + 1)
                    if n == 2:
                        pe.wait_ge(s_ev, 1)
                    for b in range(EBLK):
                        m = P if b < FULL_BLK else ET - FULL_BLK * P
                        mm = nc.tensor.transpose(ps[:, bank + b // 4, (b % 4) * P:(b % 4) * P + m],
                                                 rows_f[0:m, b * P:(b + 1) * P], ident[0:m, 0:m])
                    mm.then_inc(s_tr, 1)
                pe.wait_ge(s_ev, 3)
                first = dstT.rearrange("p (g t) -> p g t", t=EDGE_TILES)[0:1, :, 0]
                nc.tensor.matmul(ps[:, 6, 0:GROUPS], ones[0:1, :], first, start=True, stop=True).then_inc(s_base, 1)
                pe.wait_ge(s_flag, 1)
                nc.tensor.matmul(ps[0:1, 7, 0:1], ones[:, 0:1], small[:, 0:1], start=True, stop=True)\
                  .then_inc(s_flag2, 1)

            @block.vector
            def _(dve):
                v = nc.vector
                v.memset(aggT[:, :, :], 0.0)
                v.memset(small[:, :], 0.0)
                dve.wait_ge(s_load, 16 * 9)
                v.tensor_copy(row_dst, row_dst_i).then_inc(s_cast, 2)
                v.tensor_copy(row_src, row_src_i).then_inc(s_cast, 1)
                for n, dst in enumerate((dstT, ewT[:, :], srcT[:, :])):
                    dve.wait_ge(s_tr, n + 1)
                    bank = 4 * (n % 2)
                    v.tensor_copy(dst, ps[:, bank:bank + 4, :].rearrange("p a b -> p (a b)")[:, 0:ET])\
                     .then_inc(s_ev, 1)
                dve.wait_ge(s_ev, 3)
                grp = lambda a: a.rearrange("p (g t) -> p g t", t=EDGE_TILES)
                v.tensor_copy(base_i[0:1, :], grp(dstT)[0:1, :, 0])
                dve.wait_ge(s_base, 1)
                dve.wait_ge(s_c, 12)
                v.tensor_tensor(grp(dstL[:, :]), grp(dstT),
                                ps[:, 6, 0:GROUPS].unsqueeze(2).to_broadcast([P, GROUPS, EDGE_TILES]), ALU.subtract)
                v.tensor_tensor(grp(stray), grp(dstT),
                                frontier.unsqueeze(2).to_broadcast([P, GROUPS, EDGE_TILES]), ALU.is_lt)
                dve.drain()
                v.scalar_tensor_tensor(tmp_e, dstL[:, :], 0.0, stray, ALU.is_lt, ALU.max)
                dve.drain()
                v.scalar_tensor_tensor(stray, dstL[:, :], float(WIN) - 0.5, tmp_e, ALU.is_gt, ALU.max)
                dve.drain()
                v.reduce_sum(small[:, 0:1], stray, axis=AX_X).then_inc(s_flag, 1)
                v.scalar_tensor_tensor(dstL[:, :], stray, -20000.0, dstL[:, :], ALU.mult, ALU.add)
                v.scalar_tensor_tensor(tmp_e, dstT, 1.0, stray, ALU.add, ALU.mult)
                v.tensor_copy(ew3[:, :, 0], ewT[:, :])
                dve.drain()
                v.tensor_scalar(dstT, tmp_e, -1.0, None, ALU.add).then_inc(s_stray, 1)
                v.tensor_tensor(stray, ewT[:, :], ew3[:, :, 0], ALU.subtract)
                dve.drain()
                v.tensor_copy(ew3[:, :, 1], stray)
                dve.drain()
                v.tensor_tensor(tmp_e, stray, ew3[:, :, 1], ALU.subtract)
                dve.drain()
                v.tensor_copy(ew3[:, :, 2], tmp_e)
                v.tensor_scalar(before[:, :, :], before[:, :, :], 0.0, None, ALU.is_lt)
                dve.wait_ge(s_flag2, 1)
                v.tensor_copy(flag_i[0:1, 0:1], ps[0:1, 7, 0:1])

        deg3 = big[0:3, 0:NP]
        stray_dst = rows[:, 2, :, :].rearrange("p a b -> p (a b)")[:, 0:ET]
        DG = 3
        s_oh = sem("onehot_ready")
        s_dm = sem("degree_summed")
        s_dmc = sem("degree_transposed")
        s_slq = sem("slow_strays_loaded")
        s_soh = sem("slow_onehot_ready")
        s_sdm = sem("slow_degree_summed")
        iota_b = iota_w[:, :].unsqueeze(1).to_broadcast([P, EDGE_TILES, WIN])

        ew3s = small[:, 0:DG * 3 * EDGE_TILES // 2 + 1].bitcast(BF16)[:, 0:DG * 3 * EDGE_TILES]\
            .rearrange("p (s t c) -> p s t c", s=DG, c=3)

        def local(a, g):
            return a[:, bass.ds(g * EDGE_TILES, EDGE_TILES)].unsqueeze(2).to_broadcast([P, EDGE_TILES, WIN])

        with nc.Block() as block:
            @block.tensor
            def _(pe):
                with pe.Fori(0, GROUPS // DG) as i:
                    for k in range(DG):
                        pe.wait_ge(s_oh, DG * i + k + 1)
                        for t in range(EDGE_TILES):
                            mm = nc.tensor.matmul(ps[0:3, k, 0:WIN], ew3s[:, k, t, :], deg_oh[:, k, t, :],
                                                  start=(t == 0), stop=(t == EDGE_TILES - 1))
                        mm.then_inc(s_dm, 1)

            @block.vector
            def _(dve):
                v = nc.vector
                v.memset(deg3, 0.0)
                dve.drain()
                with dve.Fori(0, GROUPS // DG) as i:
                    for k in range(DG):
                        g = DG * i + k
                        v.tensor_copy(ew3s[:, k, :, :], ew3[:, bass.ds(g * EDGE_TILES, EDGE_TILES), :])
                        v.tensor_tensor(deg_oh[:, k, :, :], local(dstL, g), iota_b, ALU.is_equal)
                        dve.drain().then_inc(s_oh, 1)
                    for k in range(DG):
                        g = DG * i + k
                        b = dve.value_load(base_i[0:1, bass.ds(g, 1)], min_val=0, max_val=N - 1)
                        dve.wait_ge(s_dm, g + 1)
                        v.tensor_tensor(deg3[:, bass.ds(b, WIN)], deg3[:, bass.ds(b, WIN)], ps[0:3, k, 0:WIN], ALU.add)
                        dve.drain()

        with nc.Block() as block:
            @block.sync
            def _(sp):
                f = sp.value_load(flag_i[0:1, 0:1], min_val=0, max_val=ET * P)
                with sp.If(f != 0):
                    sp.dma_start(stray_dst, stray_dram[:, :]).then_inc(s_slq, 16)
                    sp.wait_ge(s_slq, 16)
                sp.nop()

            @block.tensor
            def _(pe):
                f = pe.value_load(flag_i[0:1, 0:1], min_val=0, max_val=ET * P)
                with pe.If(f != 0):
                    with pe.Fori(0, GROUPS) as g:
                        with pe.Fori(0, SLOW_WIN) as w:
                            pe.wait_ge(s_soh, SLOW_WIN * g + w + 1)
                            for t in range(EDGE_TILES):
                                mm = nc.tensor.matmul(ps[0:3, 0, 0:WIN], ew3s[:, 0, t, :], deg_oh[:, 0, t, :],
                                                      start=(t == 0), stop=(t == EDGE_TILES - 1))
                            mm.then_inc(s_sdm, 1)
                pe.nop()

            @block.vector
            def _(dve):
                v = nc.vector
                f = dve.value_load(flag_i[0:1, 0:1], min_val=0, max_val=ET * P)
                with dve.If(f != 0):
                    dve.wait_ge(s_slq, 16)
                    with dve.Fori(0, GROUPS) as g:
                        with dve.Fori(0, SLOW_WIN) as w:
                            v.tensor_copy(ew3s[:, 0, :, :], ew3[:, bass.ds(g * EDGE_TILES, EDGE_TILES), :])
                            v.tensor_scalar(stray_t[:, :], stray_dst[:, bass.ds(g * EDGE_TILES, EDGE_TILES)],
                                            win_start[:, bass.ds(w, 1)], None, ALU.subtract)
                            dve.drain()
                            v.tensor_tensor(deg_oh[:, 0, :, :], stray_t[:, :].unsqueeze(2)
                                            .to_broadcast([P, EDGE_TILES, WIN]), iota_b, ALU.is_equal)
                            dve.drain().then_inc(s_soh, 1)
                            dve.wait_ge(s_sdm, SLOW_WIN * g + w + 1)
                            v.tensor_tensor(deg3[:, bass.ds(w * WIN, WIN)], deg3[:, bass.ds(w * WIN, WIN)],
                                            ps[0:3, 0, 0:WIN], ALU.add)
                            dve.drain()
                dve.nop()

        s_dn = sem("degrees_by_node")
        dtmp = small[:, 0:NT]
        dpos = small[:, 64:64 + NT]
        with nc.Block() as block:
            @block.tensor
            def _(pe):
                for j in range(NT):
                    mm = nc.tensor.matmul(ps[:, 0, j:j + 1], deg3[:, j * P:(j + 1) * P], ones[0:3, 0:1],
                                          start=True, stop=True)
                mm.then_inc(s_dn, 1)

            @block.vector
            def _(dve):
                v = nc.vector
                dve.wait_ge(s_dn, 1)
                v.tensor_scalar(dtmp, ps[:, 0, 0:NT], 1.0, 1e-30, ALU.add, ALU.max)
                v.tensor_scalar(dpos, ps[:, 0, 0:NT], 1.0, 0.0, ALU.add, ALU.is_gt)
                dve.drain()
                rsqrt(dve, dinv[:, :], dtmp, small[:, 128:128 + NT])
                v.tensor_tensor(dinv[:, :], dinv[:, :], dpos, ALU.mult)

        XK = 4
        xT = big[:, 0:KH * NT * P].rearrange("p (k n) -> p k n", k=KH)
        o = KH * NT * P
        wkv = big[:, o:o + 1024].rearrange("p (k n) -> p k n", k=KH)
        wq = big[:, o + 1024:o + 1536].rearrange("p (k n) -> p k n", k=KH)
        wo = big[:, o + 1536:o + 2048].rearrange("p (k n) -> p k n", k=KH)
        kv_bd = big[:, o + 2048:o + 2304].rearrange("p (k n) -> p k n", k=KH)
        ks_bd = big[:, o + 2304:o + 2560].rearrange("p (k n) -> p k n", k=KH)
        blockdiag = big[:, o + 2560:o + 2560 + P]
        bias_kv = big[:, o + 2688:o + 2688 + 512]
        bq_col = big[:, o + 3200:o + 3202]
        bo_bc = big[:, o + 3204:o + 3204 + D]

        def pool_ring(n):
            return rows[:, n // 2, :, :].rearrange("p a b -> p (a b)")[:, (n % 2) * 1024:(n % 2 + 1) * 1024]\
                .rearrange("p (s d) -> p s d", s=XK)
        x_in, x_hat, z_row, x_tT = (pool_ring(n) for n in range(4))
        kv_raw = scratch[:, 0:2, :]
        k_neg = scratch[:, 2, :].rearrange("p (s d) -> p s d", s=2)
        k_feat = scratch[:, 3, :].rearrange("p (s d) -> p s d", s=2)
        v_one = scratch[:, 4:6, :]
        stats = small[:, 0:XK * 6].rearrange("p (s c) -> p s c", s=XK)
        mv = small[:, 32:32 + XK * 2].rearrange("p (s c) -> p s c", s=XK)
        rstd = small[:, 48:48 + XK]
        var = small[:, 52:52 + XK]

        s_w = sem("mix_weights_loaded")
        s_bd = sem("mix_constants")
        s_xl = [sem(f"x_loaded{s}") for s in range(XK)]
        s_xh = sem("x_hat_ready")
        s_z = sem("z_ready")
        s_zs = [sem(f"z_stored{s}") for s in range(XK)]
        s_xt = sem("tiles_transposed")
        s_xe = sem("transposes_evacuated")
        s_xc = sem("x_T_copied")
        s_kv = sem("kv_projected")
        s_kr = sem("kv_raw_ready")
        s_ke = sem("k_exp_ready")
        s_kf = sem("k_feature_ready")
        s_ka = sem("kv_accumulated")
        s_kd = sem("kv_read")

        def row_bc(v):
            return v.rearrange("(a n) -> a n", a=1).to_broadcast([P, v.shape[0]])

        x_tiles = A["x"]

        with nc.Block() as block:
            @block.sync
            def _(sp):
                for w, n0 in (("L0_mix_wk", 0), ("L0_mix_wv", D)):
                    sp.dma_start(wkv[:, :, n0:n0 + D], A[w].rearrange("(k p) n -> p k n", p=P)).then_inc(s_w, 16)
                sp.dma_start(bias_kv[:, 0:D], row_bc(A["L0_mix_bk"])).then_inc(s_w, 16)
                sp.dma_start(bias_kv[:, D:2 * D], row_bc(A["L0_mix_bv"])).then_inc(s_w, 16)
                sp.dma_start(wq, A["L0_mix_wq"].rearrange("(k p) n -> p k n", p=P)).then_inc(s_w, 16)
                sp.dma_start(wo, A["L0_mix_wo"].rearrange("(k p) n -> p k n", p=P)).then_inc(s_w, 16)
                sp.dma_start(bo_bc, row_bc(A["L0_mix_bo"])).then_inc(s_w, 16)
                with nc.allow_non_contiguous_dma(reason="256 biases, one per partition"):
                    sp.dma_start(bq_col, A["L0_mix_bq"].rearrange("(k p) -> p k", p=P)).then_inc(s_w, 16)

                def load(i, k, n):
                    ge(sp, s_xh, XK * (i - 1) + k + 1 if not isinstance(i, int) or i > 0 else 0)
                    sp.dma_start(x_in[0:n, k, :], x_tiles[bass.ds((XK * i + k) * P, n), :]).then_inc(s_xl[k], 16)
                for k in range(XK):
                    load(0, k, P)
                with sp.Fori(1, NT // XK) as i:
                    for k in range(XK):
                        load(i, k, P)
                load(NT // XK, 0, LAST)

            @block.gpsimd
            def _(pool):
                g = nc.gpsimd
                g.memset(blockdiag, 0.0).then_inc(s_bd, 1)
                g.memset(v_one, 1.0).then_inc(s_bd, 1)
                for h in range(P // DEPTH):
                    r = slice(h * DEPTH, (h + 1) * DEPTH)
                    pool.wait_ge(s_bd, 2 + h)
                    g.memset(blockdiag[r, r], 1.0).then_inc(s_bd, 1)

                def copy(i, k, n):
                    pool.wait_ge(s_xe, XK * i + k + 1)
                    g.tensor_copy(xT[:, :, bass.ds((XK * i + k) * P, n)], x_tT[:, k, :]
                                  .rearrange("p (k n) -> p k n", k=KH)[:, :, 0:n]).then_inc(s_xc, 1)
                with pool.Fori(0, NT // XK) as i:
                    for k in range(XK):
                        copy(i, k, P)
                copy(NT // XK, 0, LAST)

            @block.scalar
            def _(act):
                a = nc.scalar
                act.wait_ge(s_bd, 2 + P // DEPTH)

                def store_z(i, k, n):
                    j = XK * i + k
                    act.wait_ge(s_z, j + 1)
                    act.dma_start(z_dram[0][bass.ds(j * P, n), :], z_row[0:n, k, :]).then_inc(s_zs[k], 16)

                def evac(i, k, n):
                    j = XK * i + k
                    act.wait_ge(s_xt, j + 1)
                    ge(act, s_kv, j - XK + 1)
                    ge(act, s_xc, j - XK + 1)
                    a.activation(x_tT[:, k, :].rearrange("p (k n) -> p k n", k=KH)[:, :, 0:n],
                                 ps[:, k % 2, 0:256].rearrange("p (k n) -> p k n", k=KH)[:, :, 0:n], ACT.Copy)
                    a.activation(aggT[:, :, bass.ds(j * P, n)],
                                 ps[:, k % 2, 256:512].rearrange("p (k n) -> p k n", k=KH)[:, :, 0:n], ACT.Copy)\
                     .then_inc(s_xe, 1)

                def expo(i, k, n):
                    j = XK * i + k
                    act.wait_ge(s_kr, j + 1)
                    a.activation(k_neg[0:n, k % 2, :], k_neg[0:n, k % 2, :], ACT.Exp).then_inc(s_ke, 1)

                def tiles(i, ks, n):
                    for k in ks:
                        store_z(i, k, n)
                        evac(i, k, n)
                        expo(i, k, n)
                tiles(0, range(XK), P)
                with act.Fori(1, NT // XK) as i:
                    tiles(i, range(XK), P)
                tiles(NT // XK, range(1), LAST)
                for k in range(XK):
                    act.wait_ge(s_zs[k], 16 * (NT // XK + (k == 0)))

            @block.vector
            def _(dve):
                v = nc.vector
                dve.wait_ge(s_w, 16 * 8)
                dve.wait_ge(s_bd, 2 + P // DEPTH)

                def norm(i, ks, n):
                    for k in ks:
                        dve.wait_ge(s_xl[k], 16 * (i + 1))
                        v.bn_stats(stats[0:n, k, :], x_in[0:n, k, :])
                    dve.drain()
                    for k in ks:
                        v.bn_aggr(mv[0:n, k, :], stats[0:n, k, :])
                    dve.drain()
                    v.tensor_scalar(var[0:n, 0:len(ks)], mv[0:n, 0:len(ks), 1], EPS, None, ALU.add)
                    dve.drain()
                    rsqrt(dve, rstd[0:n, 0:len(ks)], var[0:n, 0:len(ks)], small[0:n, 56:56 + len(ks)])
                    for k in ks:
                        j = XK * i + k
                        ge(dve, s_xt, j - XK + 1)
                        v.tensor_scalar(x_hat[0:n, k, :], x_in[0:n, k, :], mv[0:n, k, 0:1], rstd[0:n, k:k + 1],
                                        ALU.subtract, ALU.mult).then_inc(s_xh, 1)
                    dve.drain()
                    for k in ks:
                        ge(dve, s_zs[k], 16 * i)
                        v.tensor_scalar(z_row[0:n, k, :], x_hat[0:n, k, :], dinv[0:n, bass.ds(XK * i + k, 1)],
                                        None, ALU.mult).then_inc(s_z, 1)

                def keys(i, k, n):
                    j = XK * i + k
                    b = k % 2
                    dve.wait_ge(s_kv, j + 1)
                    ge(dve, s_ka, j - 1)
                    v.tensor_tensor(kv_raw[0:n, b, :], ps[0:n, 2 + b, :], bias_kv[0:n, :], ALU.add)
                    dve.drain()
                    v.tensor_scalar(k_neg[0:n, b, :], kv_raw[0:n, b, 0:D], 0.0, None, ALU.min).then_inc(s_kr, 1)
                    v.tensor_copy(v_one[0:n, b, 0:2 * 129].rearrange("p (k m) -> p k m", k=KH)[:, :, 0:P],
                                  kv_raw[0:n, b, D:2 * D].rearrange("p (k m) -> p k m", k=KH))
                    dve.wait_ge(s_ke, j + 1)
                    v.scalar_tensor_tensor(k_feat[0:n, b, :], kv_raw[0:n, b, 0:D], 0.0, k_neg[0:n, b, :],
                                           ALU.max, ALU.add)
                    dve.drain().then_inc(s_kf, 1)

                def tiles(i, ks, n):
                    norm(i, ks, n)
                    for k in ks:
                        keys(i, k, n)
                tiles(0, range(XK), P)
                with dve.Fori(1, NT // XK) as i:
                    tiles(i, range(XK), P)
                tiles(NT // XK, range(1), LAST)
                dve.wait_ge(s_ka, NT)
                for a in range(KH):
                    v.tensor_tensor(kv_bd[:, a, :], ps[:, 6 + a, 0:P], blockdiag, ALU.mult)
                    v.tensor_copy(small[:, 64 + a:65 + a], ps[:, 6 + a, P:P + 1])
                dve.drain()
                for a in range(KH):
                    v.tensor_scalar(ks_bd[:, a, :], blockdiag, small[:, 64 + a:65 + a], None, ALU.mult)

            @block.tensor
            def _(pe):
                t = nc.tensor
                pe.wait_ge(s_w, 16 * 8)

                def trans(i, k, n):
                    j = XK * i + k
                    pe.wait_ge(s_z, j + 1)
                    ge(pe, s_xe, j - 1)
                    for m, src in enumerate((x_hat, z_row)):
                        for h in range(KH):
                            mm = t.transpose(ps[:, k % 2, m * 256 + h * P:m * 256 + h * P + n],
                                             src[0:n, k, h * P:(h + 1) * P], ident[0:n, 0:n])
                    mm.then_inc(s_xt, 1)

                def project(i, k, n):
                    j = XK * i + k
                    pe.wait_ge(s_xe, j + 1)
                    ge(pe, s_kf, j - 1)
                    for h in range(KH):
                        mm = t.matmul(ps[0:n, 2 + k % 2, :], x_tT[:, k, h * P:h * P + n], wkv[:, h, :],
                                      start=(h == 0), stop=(h == KH - 1))
                    mm.then_inc(s_kv, 1)

                def accumulate(i, k, n, first, last):
                    j = XK * i + k
                    pe.wait_ge(s_kf, j + 1)
                    for a in range(KH):
                        mm = t.matmul(ps[:, 6 + a, 0:129], k_feat[0:n, k % 2, a * P:(a + 1) * P],
                                      v_one[0:n, k % 2, a * 129:(a + 1) * 129], start=first, stop=last,
                                      skip_group_check=True)
                    mm.then_inc(s_ka, 1)

                def tiles(i, ks, n, first=False, last=False):
                    for k in ks:
                        trans(i, k, n)
                        project(i, k, n)
                        accumulate(i, k, n, first and k == 0, last and k == ks[-1])
                tiles(0, range(XK), P, first=True)
                with pe.Fori(1, NT // XK) as i:
                    tiles(i, range(XK), P)
                tiles(NT // XK, range(1), LAST, last=True)

        s_q = sem("q_projected")
        s_qm = sem("q_min_ready")
        s_qx = sem("q_exp_ready")
        s_qf = sem("q_feature_ready")
        s_o = sem("attention_done")
        s_on = sem("attention_normalised")
        s_m = sem("mix_projected")
        s_r = sem("residual_ready")
        s_rx = [sem(f"x_reloaded{k}") for k in range(2)]
        s_rs = [sem(f"residual_stored{k}") for k in range(2)]
        q_neg = halves(piece(0))
        q_pos = halves(piece(1))
        q_feat = halves(piece(2))
        o_norm = halves(piece(3))
        o_T = halves(piece(4))
        x_again = [halves(piece(5 + k)) for k in range(2)]
        res_out = [halves(piece(7 + k)) for k in range(2)]
        FULL_CH = N // CH

        with nc.Block() as block:
            @block.sync
            def _(sp):
                def load(c, b):
                    ge(sp, s_r, c - 1)
                    sp.dma_start(x_again[b], x_tiles[bass.ds(c * CH, CH), :].rearrange("(j p) d -> p j d", p=P))\
                      .then_inc(s_rx[b], 16)

                def store(c, b):
                    sp.wait_ge(s_r, c + 1)
                    sp.dma_start(res_dram[bass.ds(c * CH, CH), :].rearrange("(j p) d -> p j d", p=P), res_out[b])\
                      .then_inc(s_rs[b], 16)
                load(0, 0)
                load(1, 1)
                with sp.Fori(0, FULL_CH // 2 - 1) as i:
                    for b in range(2):
                        store(2 * i + b, b)
                        load(2 * i + 2 + b, b)
                for b in range(2):
                    store(FULL_CH - 2 + b, b)
                sp.wait_ge(s_r, FULL_CH - 1)
                sp.dma_start(x_again[0][0:LAST, 0, :], x_tiles[FULL_CH * CH:N, :]).then_inc(s_rx[0], 16)
                sp.wait_ge(s_r, FULL_CH + 1)
                sp.dma_start(res_dram[FULL_CH * CH:N, :], res_out[0][0:LAST, 0, :]).then_inc(s_rs[0], 16)
                sp.wait_ge(s_rs[0], 16 * (FULL_CH // 2 + 1))
                sp.wait_ge(s_rs[1], 16 * (FULL_CH // 2))

            @block.tensor
            def _(pe):
                t = nc.tensor

                def chunk(c, n):
                    ge(pe, s_qm, c)
                    for a in range(KH):
                        for h in range(KH):
                            mm = t.matmul(ps[:, 0, a * 256:a * 256 + n], wq[:, h, a * P:(a + 1) * P],
                                          xT[:, h, bass.ds(c * CH, n)], start=(h == 0), stop=(h == KH - 1))
                    mm.then_inc(s_q, 1)
                    pe.wait_ge(s_qf, c + 1)
                    ge(pe, s_on, c)
                    for bank, w in ((1, kv_bd), (2, ks_bd)):
                        for a in range(KH):
                            mm = t.matmul(ps[:, bank, a * 256:a * 256 + n], w[:, a, :], q_feat[:, a, 0:n],
                                          start=True, stop=True)
                    mm.then_inc(s_o, 1)
                    pe.wait_ge(s_on, c + 1)
                    ge(pe, s_r, c)
                    for j in range(-(-n // P)):
                        m = min(P, n - j * P)
                        for a in range(KH):
                            mm = t.matmul(ps[0:m, 3, j * 256:(j + 1) * 256], o_T[:, a, j * P:j * P + m], wo[:, a, :],
                                          start=(a == 0), stop=(a == KH - 1))
                    mm.then_inc(s_m, 1)
                chunk(0, CH)
                with pe.Fori(1, FULL_CH) as c:
                    chunk(c, CH)
                chunk(FULL_CH, LAST)

            @block.scalar
            def _(act):
                def chunk(c, n):
                    act.wait_ge(s_qm, c + 1)
                    nc.scalar.activation(q_neg[:, :, 0:n], q_neg[:, :, 0:n], ACT.Exp).then_inc(s_qx, 1)
                with act.Fori(0, FULL_CH) as c:
                    chunk(c, CH)
                chunk(FULL_CH, LAST)

            @block.vector
            def _(dve):
                v = nc.vector

                def chunk(c, b, n, i):
                    dve.wait_ge(s_q, c + 1)
                    for a in range(KH):
                        src = ps[:, 0, a * 256:a * 256 + n]
                        v.tensor_scalar(q_pos[:, a, 0:n], src, bq_col[:, a:a + 1], 0.0, ALU.add, ALU.max)
                        mn = v.tensor_scalar(q_neg[:, a, 0:n], src, bq_col[:, a:a + 1], 0.0, ALU.add, ALU.min)
                    mn.then_inc(s_qm, 1)
                    dve.wait_ge(s_qx, c + 1)
                    v.tensor_tensor(q_feat[:, :, 0:n], q_pos[:, :, 0:n], q_neg[:, :, 0:n], ALU.add)\
                     .then_inc(s_qf, 1)
                    dve.wait_ge(s_o, c + 1)
                    two = lambda bank: halves(ps[:, bank, :])[:, :, 0:n]
                    v.tensor_scalar(o_norm[:, :, 0:n], two(2), 1e-6, None, ALU.add)
                    dve.drain()
                    v.reciprocal(o_norm[:, :, 0:n], o_norm[:, :, 0:n])
                    dve.drain()
                    v.tensor_tensor(o_T[:, :, 0:n], two(1), o_norm[:, :, 0:n], ALU.mult).then_inc(s_on, 1)
                    dve.wait_ge(s_rx[b], 16 * (i + 1))
                    ge(dve, s_rs[b], 16 * i)
                    dve.wait_ge(s_m, c + 1)
                    m = min(n, P)
                    nj = -(-n // P)
                    v.tensor_tensor(res_out[b][0:m, 0:nj, :], halves(ps[0:m, 3, :])[:, 0:nj, :],
                                    x_again[b][0:m, 0:nj, :], ALU.add)
                    dve.drain()
                    v.tensor_tensor(res_out[b][0:m, 0:nj, :], res_out[b][0:m, 0:nj, :],
                                    bo_bc[0:m, :].unsqueeze(1).to_broadcast([m, nj, D]), ALU.add).then_inc(s_r, 1)
                for b in range(2):
                    chunk(b, b, CH, 0)
                with dve.Fori(1, FULL_CH // 2) as i:
                    for b in range(2):
                        chunk(2 * i + b, b, CH, i)
                chunk(FULL_CH, 0, LAST, FULL_CH // 2)

        def stray_path(layer):
            s_l = sem(f"strays_loaded{layer}")
            s_i = sem(f"stray_idx_staged{layer}")
            s_b = sem(f"stray_gathers_begun{layer}")
            s_g = sem(f"stray_rows_gathered{layer}")
            s_s = sem(f"stray_S_ready{layer}")
            s_mm = sem(f"stray_summed{layer}")
            s_f = sem(f"stray_rows_free{layer}")
            with nc.Block() as block:
                @block.sync
                def _(sp):
                    f = sp.value_load(flag_i[0:1, 0:1], min_val=0, max_val=ET * P)
                    with sp.If(f != 0):
                        sp.dma_start(stray_dst, stray_dram[:, :]).then_inc(s_l, 16)
                        sp.wait_ge(s_l, 16)
                    sp.nop()

                @block.gpsimd
                def _(pool):
                    f = pool.value_load(flag_i[0:1, 0:1], min_val=0, max_val=ET * P)
                    with pool.If(f != 0):
                        with pool.Fori(0, GROUPS) as g:
                            pool.wait_ge(s_f, g + 1)
                            nc.gpsimd.tensor_copy(idx[:, 0, :], srcT[:, bass.ds(g * EDGE_TILES, EDGE_TILES)])\
                              .then_inc(s_i, 1)
                            pool.wait_ge(s_i, g + 1)
                            pool.sem_inc(s_b, 1)
                            for t in range(EDGE_TILES):
                                pool.indirect_dma_start(
                                    out=rows[:, 0, t, :], out_offset=None, in_=z_dram[layer][:, :],
                                    in_offset=bass.IndirectOffsetOnAxis(ap=idx[:, 0, t:t + 1], axis=0))\
                                    .then_inc(s_g, 16)
                    pool.nop()

                @block.tensor
                def _(pe):
                    f = pe.value_load(flag_i[0:1, 0:1], min_val=0, max_val=ET * P)
                    with pe.If(f != 0):
                        with pe.Fori(0, GROUPS) as g:
                            with pe.Fori(0, SLOW_WIN) as w:
                                pe.wait_ge(s_g, GATHER_INC * (g + 1))
                                pe.wait_ge(s_s, SLOW_WIN * g + w + 1)
                                for h in range(KH):
                                    for t in range(EDGE_TILES):
                                        mm = nc.tensor.matmul(ps[:, 0, h * WIN:(h + 1) * WIN],
                                                              rows[:, 0, t, h * P:(h + 1) * P], S[:, 0, t, :],
                                                              start=(t == 0), stop=(t == EDGE_TILES - 1))
                                mm.then_inc(s_mm, 1)
                    pe.nop()

                @block.vector
                def _(dve):
                    v = nc.vector
                    f = dve.value_load(flag_i[0:1, 0:1], min_val=0, max_val=ET * P)
                    with dve.If(f != 0):
                        dve.wait_ge(s_l, 16)
                        with dve.Fori(0, GROUPS) as g:
                            dve.sem_inc(s_f, 1)
                            with dve.Fori(0, SLOW_WIN) as w:
                                v.tensor_scalar(stray_t[:, :], stray_dst[:, bass.ds(g * EDGE_TILES, EDGE_TILES)],
                                                win_start[:, bass.ds(w, 1)], None, ALU.subtract)
                                dve.drain()
                                v.tensor_tensor(S[:, 0, :, :], stray_t[:, :].unsqueeze(2)
                                                .to_broadcast([P, EDGE_TILES, WIN]), iota_b, ALU.is_equal)
                                dve.drain()
                                v.tensor_tensor(S[:, 0, :, :], S[:, 0, :, :], local(ewT, g), ALU.mult)\
                                 .then_inc(s_s, 1)
                                dve.wait_ge(s_mm, SLOW_WIN * g + w + 1)
                                v.tensor_tensor(aggT[:, :, bass.ds(w * WIN, WIN)], aggT[:, :, bass.ds(w * WIN, WIN)],
                                                ps[:, 0, 0:KH * WIN].rearrange("p (k w) -> p k w", k=KH), ALU.add)
                                dve.drain()
                    dve.nop()

        class Agg:

            def __init__(self, layer):
                self.z = z_dram[layer]
                self.staged = sem(f"idx_staged{layer}")
                self.begun = sem(f"gathers_begun{layer}")
                self.gathered = [sem(f"rows_gathered{layer}_{s}") for s in range(RING)]
                self.s_ready = sem(f"S_ready{layer}")
                self.done = sem(f"group_summed{layer}")
                self.evac = sem(f"group_added{layer}")

            def pool(self, pool, it, k):
                g, s = GI * it + k, k % RING
                ge(pool, self.done, g - RING + 1)
                nc.gpsimd.tensor_copy(idx[:, s, :], srcT[:, bass.ds(g * EDGE_TILES, EDGE_TILES)])\
                  .then_inc(self.staged, 1)
                pool.wait_ge(self.staged, g + 1)
                pool.sem_inc(self.begun, 1)
                for t in range(EDGE_TILES):
                    pool.indirect_dma_start(out=rows[:, s, t, :], out_offset=None, in_=self.z[:, :],
                                            in_offset=bass.IndirectOffsetOnAxis(ap=idx[:, s, t:t + 1], axis=0))\
                        .then_inc(self.gathered[s], 16)

            def pe(self, pe, it, k):
                g, s, b = GI * it + k, k % RING, k % 2
                pe.wait_ge(self.s_ready, g + 1)
                ge(pe, self.evac, g - 1)
                pe.wait_ge(self.gathered[s], GATHER_INC * (GI // RING * it + k // RING + 1))
                for h in range(KH):
                    for t in range(EDGE_TILES):
                        mm = nc.tensor.matmul(ps[:, b, h * WIN:(h + 1) * WIN], rows[:, s, t, h * P:(h + 1) * P],
                                              S[:, b, t, :], start=(t == 0), stop=(t == EDGE_TILES - 1))
                mm.then_inc(self.done, 1)

            def make_s(self, dve, it, k):
                g, b = GI * it + k, k % 2
                ge(dve, self.done, g - 1)
                nc.vector.tensor_tensor(S[:, b, :, :], local(dstL, g), iota_b, ALU.is_equal)
                dve.drain()
                nc.vector.tensor_tensor(S[:, b, :, :], S[:, b, :, :], local(ewT, g), ALU.mult)\
                  .then_inc(self.s_ready, 1)

            def add(self, dve, it, k):
                g, b = GI * it + k, k % 2
                base = dve.value_load(base_i[0:1, bass.ds(g, 1)], min_val=0, max_val=N - 1)
                dve.wait_ge(self.done, g + 1)
                nc.vector.tensor_tensor(aggT[:, :, bass.ds(base, WIN)], aggT[:, :, bass.ds(base, WIN)],
                                        ps[:, b, 0:KH * WIN].rearrange("p (k w) -> p k w", k=KH), ALU.add)
                dve.drain().then_inc(self.evac, 1)

            def dve(self, dve, it, k, last):
                if not last:
                    self.make_s(dve, it, k + 1)
                self.add(dve, it, k)

        staged = halves(piece(9))
        gcn_w = halves(piece(10))
        gcn_b = piece(11)[:, 0:D]
        FULL_CHUNKS = CHUNKS - 1

        stray_path(0)
        l1 = Agg(0)
        s_gw = sem("gcn1_weights_loaded")
        s_st = sem("chunk_staged1")
        s_gm = sem("chunk_projected1")
        s_t1 = sem("chunk_biased1")
        s_z2 = sem("z2_ready")
        s_z2s = sem("z2_stored")
        s_z2t = sem("z2_transposed")
        s_z2c = sem("z2_in_aggT")
        h_pre = halves(piece(0))
        z2 = halves(piece(1))
        FFW = 4
        s_ffw = sem("ffn_weights_loaded")

        with nc.Block() as block:
            @block.gpsimd
            def _(pool):
                for k in range(GI):
                    l1.pool(pool, 0, k)
                with pool.Fori(1, ITERS) as it:
                    for k in range(GI):
                        l1.pool(pool, it, k)
                for k in range(G_REST):
                    l1.pool(pool, ITERS, k)

            @block.sync
            def _(sp):
                sp.dma_start(gcn_w, A["L0_gnn_W1"].rearrange("(k p) n -> p k n", p=P)).then_inc(s_gw, 16)
                sp.dma_start(gcn_b, row_bc(A["L0_gnn_b1"])).then_inc(s_gw, 16)
                with sp.Fori(0, FULL_CHUNKS) as c:
                    sp.wait_ge(s_z2, c + 1)
                    sp.dma_start(z_dram[1][bass.ds(c * CH, CH), :].rearrange("(j p) d -> p j d", p=P), z2)\
                      .then_inc(s_z2s, 16)
                sp.wait_ge(s_z2, CHUNKS)
                sp.dma_start(z_dram[1][FULL_CHUNKS * CH:N, :], z2[0:LAST, 0, :]).then_inc(s_z2s, 16)
                sp.wait_ge(s_z2s, 16 * CHUNKS)

            @block.tensor
            def _(pe):
                t = nc.tensor
                pe.wait_ge(s_gw, 32)

                def post(c, nj, m):
                    pe.wait_ge(s_st, c + 1)
                    ge(pe, s_t1, c)
                    for j in range(nj):
                        for h in range(KH):
                            mm = t.matmul(ps[:, 6, j * 256:(j + 1) * 256], staged[:, h, j * P:(j + 1) * P],
                                          gcn_w[:, h, :], start=(h == 0), stop=(h == KH - 1))
                    mm.then_inc(s_gm, 1)
                    pe.wait_ge(s_z2, c + 1)
                    ge(pe, s_z2c, c)
                    for j in range(nj):
                        for h in range(KH):
                            mm = t.transpose(ps[:, 7, h * 256 + j * P:h * 256 + j * P + m],
                                             z2[0:m, j, h * P:(h + 1) * P], ident[0:m, 0:m])
                    mm.then_inc(s_z2t, 1)

                def iteration(it):
                    for k in range(GI):
                        l1.pe(pe, it, k)
                        if k == PRE_STEP and not (isinstance(it, int) and it == 0):
                            post(it - 1, 2, P)
                iteration(0)
                iteration(1)
                with pe.Fori(2, ITERS) as it:
                    iteration(it)
                for k in range(G_REST):
                    l1.pe(pe, ITERS, k)
                    if k == PRE_STEP:
                        post(ITERS - 1, 2, P)
                post(ITERS, 1, LAST)

            @block.scalar
            def _(act):
                def chunk(c, nj, m):
                    act.wait_ge(s_t1, c + 1)
                    ge(act, s_z2s, 16 * c)
                    ge(act, s_z2t, c)
                    for j in range(nj):
                        a = nc.scalar.activation(z2[0:m, j, :], h_pre[0:m, j, :], ACT.Relu,
                                                 scale=dinv[0:m, bass.ds(2 * c + j, 1)])
                    a.then_inc(s_z2, 1)
                chunk(0, 2, P)
                with act.Fori(1, FULL_CHUNKS) as c:
                    chunk(c, 2, P)
                chunk(FULL_CHUNKS, 1, LAST)

            @block.vector
            def _(dve):
                v = nc.vector
                dve.wait_ge(s_gw, 32)

                def post(c, nj, m):
                    ge(dve, s_gm, c)
                    v.tensor_scalar(staged[:, :, 0:nj * P], aggT[:, :, bass.ds(c * CH, nj * P)], 1.0, None, ALU.mult)
                    dve.drain().then_inc(s_st, 1)
                    dve.wait_ge(s_gm, c + 1)
                    ge(dve, s_z2, c)
                    for j in range(nj):
                        v.scalar_tensor_tensor(h_pre[:, j, :], ps[:, 6, j * 256:(j + 1) * 256],
                                               dinv[:, bass.ds(2 * c + j, 1)], gcn_b, ALU.mult, ALU.add)
                    dve.drain().then_inc(s_t1, 1)
                    dve.wait_ge(s_z2t, c + 1)
                    n = (nj - 1) * P + m
                    v.tensor_scalar(aggT[:, :, bass.ds(c * CH, n)], halves(ps[:, 7, :])[:, :, 0:n], 1.0, None, ALU.mult)
                    dve.drain().then_inc(s_z2c, 1)

                l1.make_s(dve, 0, 0)

                def iteration(it):
                    for k in range(GI):
                        l1.dve(dve, it, k, False)
                        if k == PRE_STEP and not (isinstance(it, int) and it == 0):
                            post(it - 1, 2, P)
                iteration(0)
                iteration(1)
                with dve.Fori(2, ITERS) as it:
                    iteration(it)
                for k in range(G_REST):
                    l1.dve(dve, ITERS, k, k == G_REST - 1)
                    if k == PRE_STEP:
                        post(ITERS - 1, 2, P)
                post(ITERS, 1, LAST)

        w1 = big[:, 0:KH * NE * H].rearrange("p (k e h) -> p k e h", k=KH, e=NE)
        w2 = big[:, KH * NE * H:].rearrange("p (e c o) -> p e c o", e=NE, c=HC)
        hT = [scratch[:, 2 * b:2 * b + 2, :].rearrange("p a b -> p (a b)").rearrange("p (c n) -> p c n", c=HC)
              for b in range(2)]
        res_in = halves(piece(4))
        x2 = halves(piece(5))
        xn = halves(piece(6))
        xnT = halves(piece(7))
        y_acc = halves(piece(8))
        y_out = halves(piece(12))
        b2_sb = piece(11)[0:NE, D:2 * D]
        wT = piece(13)[0:NE, 0:CH]
        cmp = piece(13)[:, 256:256 + 128].rearrange("p (j e f) -> p j e f", j=2, e=NE)
        sm = lambda a, n: small[:, a:a + n]
        b1_col = sm(0, NE * HC)
        gam_col, bet_col = sm(32, 2), sm(34, 2)
        wr = sm(36, 16).rearrange("p (k e) -> p k e", k=KH)
        br_bc = sm(52, NE)
        st2 = sm(60, 12).rearrange("p (j c) -> p j c", j=2)
        mv2 = sm(72, 4).rearrange("p (j c) -> p j c", j=2)
        rs2 = sm(76, 2)
        var2 = sm(164, 2)
        logit = sm(78, 16).rearrange("p (j e) -> p j e", j=2)
        rank = sm(94, 16).rearrange("p (j e) -> p j e", j=2)
        top = sm(110, 16).rearrange("p (j e) -> p j e", j=2)
        gap = sm(126, 2)
        w_top = sm(128, 4).rearrange("p (a j) -> p a j", a=2)
        w_full = sm(132, 16).rearrange("p (j e) -> p j e", j=2)
        w_tmp = sm(148, 16).rearrange("p (j e) -> p j e", j=2)
        cmp2 = piece(13)[:, 384:384 + 128].rearrange("p (j e f) -> p j e f", j=2, e=NE)

        s_fw = sem("ffn_constants_loaded")
        with nc.Block() as block:
            @block.sync
            def _(sp):
                for h in range(KH):
                    sp.dma_start(w1[:, h, :, :], A["L0_ffn_W1"][:, h * P:(h + 1) * P, :].rearrange("e p h -> p e h"))\
                      .then_inc(s_fw, 16)
                sp.dma_start(w2.rearrange("p e c o -> p (e c) o"),
                             A["L0_ffn_W2"].rearrange("e (c p) o -> p (e c) o", p=P)).then_inc(s_fw, 16)
                sp.dma_start(gcn_w, A["L0_gnn_W2"].rearrange("(k p) n -> p k n", p=P)).then_inc(s_fw, 16)
                sp.dma_start(gcn_b, row_bc(A["L0_gnn_b2"])).then_inc(s_fw, 16)
                sp.dma_start(b2_sb, A["L0_ffn_b2"]).then_inc(s_fw, 16)
                sp.dma_start(wr, A["L0_ffn_Wr"].rearrange("(k p) e -> p k e", p=P)).then_inc(s_fw, 16)
                sp.dma_start(br_bc, row_bc(A["L0_ffn_br"])).then_inc(s_fw, 16)
                with nc.allow_non_contiguous_dma(reason="vectors with one element per partition"):
                    sp.dma_start(b1_col, A["L0_ffn_b1"].rearrange("e (c p) -> p (e c)", p=P)).then_inc(s_fw, 16)
                    sp.dma_start(gam_col, A["L0_ffn_gamma"].rearrange("(k p) -> p k", p=P)).then_inc(s_fw, 16)
                    sp.dma_start(bet_col, A["L0_ffn_beta"].rearrange("(k p) -> p k", p=P)).then_inc(s_fw, 16)
                sp.wait_ge(s_fw, 16 * 11)

        stray_path(1)
        l2 = Agg(1)
        s_rl = sem("residual_loaded")
        s_st = sem("chunk_staged2")
        s_gm = sem("chunk_projected2")
        s_x2 = sem("x2_ready")
        s_xn = sem("xn_ready")
        s_xnp = sem("xn_transposed")
        s_xnt = sem("xnT_ready")
        s_lg = sem("logits_done")
        s_gap = sem("top_gap_ready")
        s_th = sem("top_tanh_ready")
        s_wf = sem("expert_weights_ready")
        s_wt = sem("expert_weights_transposed")
        s_wc = sem("expert_weights_T_ready")
        s_yb = sem("expert_bias_done")
        s_yb_read = sem("expert_bias_read")
        s_hd = sem("hidden_projected")
        s_ge = sem("gelu_done")
        s_yd = sem("expert_projected")
        s_ya = sem("expert_added")
        s_yo = sem("chunk_out_ready")
        s_ys = sem("chunk_stored")
        STEP_EXPERTS = {0: (5,), 3: (1, 2), 4: (3,), 5: (4,)}

        class Chunk:

            def __init__(self, c):
                self.c = c
                whole = not isinstance(c, int) or c < FULL_CHUNKS
                self.nj = 2 if whole else 1
                self.m = P if whole else LAST
                self.n = self.nj * P

        with nc.Block() as block:
            @block.gpsimd
            def _(pool):
                for k in range(GI):
                    l2.pool(pool, 0, k)
                with pool.Fori(1, ITERS) as it:
                    for k in range(GI):
                        l2.pool(pool, it, k)
                for k in range(G_REST):
                    l2.pool(pool, ITERS, k)

            def over_iterations(eng, step):
                for k in range(GI):
                    step(0, k, True, None, None)
                for k in range(GI):
                    step(1, k, True, None, Chunk(0))
                for k in range(GI):
                    step(2, k, True, Chunk(0), Chunk(1))
                with eng.Fori(3, ITERS) as it:
                    for k in range(GI):
                        step(it, k, True, Chunk(it - 2), Chunk(it - 1))
                for k in range(GI):
                    step(ITERS, k, k < G_REST, Chunk(ITERS - 2), Chunk(ITERS - 1))
                for k in range(GI):
                    step(ITERS + 1, k, False, Chunk(ITERS - 1), Chunk(ITERS))
                for k in range(PRE_STEP + 2):
                    step(ITERS + 2, k, False, Chunk(ITERS), None)

            @block.sync
            def _(sp):
                def load(c, nj, m):
                    ge(sp, s_x2, c)
                    if nj == 2:
                        sp.dma_start(res_in, res_dram[bass.ds(c * CH, CH), :].rearrange("(j p) d -> p j d", p=P))\
                          .then_inc(s_rl, 16)
                    else:
                        sp.dma_start(res_in[0:m, 0, :], res_dram[c * CH:N, :]).then_inc(s_rl, 16)

                def store(c, nj, m):
                    sp.wait_ge(s_yo, c + 1)
                    if nj == 2:
                        sp.dma_start(out[bass.ds(c * CH, CH), :].rearrange("(j p) d -> p j d", p=P), y_out)\
                          .then_inc(s_ys, 16)
                    else:
                        sp.dma_start(out[c * CH:N, :], y_out[0:m, 0, :]).then_inc(s_ys, 16)
                load(0, 2, P)
                load(1, 2, P)
                with sp.Fori(0, FULL_CHUNKS - 2) as c:
                    store(c, 2, P)
                    load(c + 2, 2, P)
                store(FULL_CHUNKS - 2, 2, P)
                load(FULL_CHUNKS, 1, LAST)
                store(FULL_CHUNKS - 1, 2, P)
                store(FULL_CHUNKS, 1, LAST)
                sp.wait_ge(s_ys, 16 * CHUNKS)

            @block.tensor
            def _(pe):
                t = nc.tensor

                def up(ch, e):
                    x = NE * ch.c + e
                    for c in range(HC):
                        if c % 2 == 0:
                            ge(pe, s_ge, 2 * x - 1 + c // 2)
                        for h in range(KH):
                            mm = t.matmul(ps[:, 2 + c // 2, (c % 2) * 256:(c % 2) * 256 + ch.n],
                                          w1[:, h, e, c * P:(c + 1) * P], xnT[:, h, 0:ch.n],
                                          start=(h == 0), stop=(h == KH - 1))
                        if c % 2:
                            mm.then_inc(s_hd, 1)

                def down(ch, e):
                    x = NE * ch.c + e
                    b = e % 2
                    pe.wait_ge(s_ge, 2 * x + 2)
                    ge(pe, s_ya, x - 1)
                    for j in range(ch.nj):
                        for c in range(HC):
                            mm = t.matmul(ps[:, 4 + b, j * 256:(j + 1) * 256], hT[b][:, c, j * P:(j + 1) * P],
                                          w2[:, e, c, :], start=(c == 0), stop=(c == HC - 1))
                    mm.then_inc(s_yd, 1)

                def expert(ch, e):
                    up(ch, e)
                    down(ch, e - 1)

                def gcn(ch):
                    pe.wait_ge(s_st, ch.c + 1)
                    ge(pe, s_yb_read, ch.c)
                    for j in range(ch.nj):
                        for h in range(KH):
                            mm = t.matmul(ps[:, 6, j * 256:(j + 1) * 256], staged[:, h, j * P:(j + 1) * P],
                                          gcn_w[:, h, :], start=(h == 0), stop=(h == KH - 1))
                    mm.then_inc(s_gm, 1)

                def transpose_xn(ch):
                    pe.wait_ge(s_xn, ch.c + 1)
                    ge(pe, s_wc, ch.c)
                    for j in range(ch.nj):
                        for h in range(KH):
                            mm = t.transpose(ps[:, 7, h * 256 + j * P:h * 256 + (j + 1) * P],
                                             xn[:, j, h * P:(h + 1) * P], ident[:, :])
                    mm.then_inc(s_xnp, 1)

                def logits(ch):
                    pe.wait_ge(s_xnt, ch.c + 1)
                    for j in range(ch.nj):
                        for h in range(KH):
                            mm = t.matmul(ps[:, 6, j * NE:(j + 1) * NE], xnT[:, h, j * P:(j + 1) * P], wr[:, h, :],
                                          start=(h == 0), stop=(h == KH - 1))
                    mm.then_inc(s_lg, 1)

                def bias(ch):
                    pe.wait_ge(s_wf, ch.c + 1)
                    for j in range(ch.nj):
                        mm = t.transpose(ps[0:NE, 7, j * P:(j + 1) * P], w_full[:, j, :], ident[:, :])
                    mm.then_inc(s_wt, 1)
                    pe.wait_ge(s_wc, ch.c + 1)
                    for j in range(ch.nj):
                        mm = t.matmul(ps[:, 6, j * 256:(j + 1) * 256], wT[:, j * P:(j + 1) * P], b2_sb,
                                      start=True, stop=True)
                    mm.then_inc(s_yb, 1)

                def step(it, k, agg, prev, cur):
                    if agg:
                        l2.pe(pe, it, k)
                    if k == 0 and prev:
                        expert(prev, 5)
                    if k == PRE_STEP:
                        if prev:
                            expert(prev, 6)
                        if cur:
                            gcn(cur)
                        if prev:
                            expert(prev, 7)
                        if cur:
                            transpose_xn(cur)
                    if k == PRE_STEP + 1:
                        if prev:
                            down(prev, 7)
                        if cur:
                            logits(cur)
                            up(cur, 0)
                            bias(cur)
                    if k > PRE_STEP + 1 and cur:
                        for e in STEP_EXPERTS[k]:
                            expert(cur, e)
                over_iterations(pe, step)

            @block.scalar
            def _(act):
                a = nc.scalar

                def gelu(ch, e):
                    x = NE * ch.c + e
                    ge(act, s_yd, x - 1)
                    for c in range(HC):
                        if c % 2 == 0:
                            act.wait_ge(s_hd, 2 * x + c // 2 + 1)
                        last = a.activation(hT[e % 2][:, c, 0:ch.n], ps[:, 2 + c // 2, (c % 2) * 256:(c % 2) * 256 + ch.n],
                                            ACT.Gelu, bias=b1_col[:, e * HC + c:e * HC + c + 1])
                        if c % 2:
                            last.then_inc(s_ge, 1)

                def evac_xn(ch):
                    act.wait_ge(s_xnp, ch.c + 1)
                    for h in range(KH):
                        last = a.activation(xnT[:, h, 0:ch.n], ps[:, 7, h * 256:h * 256 + ch.n], ACT.Identity,
                                            bias=bet_col[:, h:h + 1], scale=gam_col[:, h:h + 1])
                    last.then_inc(s_xnt, 1)

                def softmax(ch):
                    act.wait_ge(s_gap, ch.c + 1)
                    a.activation(gap[:, :], gap[:, :], ACT.Tanh, scale=0.5).then_inc(s_th, 1)

                def step(it, k, agg, prev, cur):
                    if k == 0 and prev:
                        gelu(prev, 5)
                    if k == PRE_STEP:
                        if prev:
                            gelu(prev, 6)
                            gelu(prev, 7)
                        if cur:
                            evac_xn(cur)
                    if k == PRE_STEP + 1 and cur:
                        softmax(cur)
                        gelu(cur, 0)
                    if k > PRE_STEP + 1 and cur:
                        for e in STEP_EXPERTS[k]:
                            gelu(cur, e)
                over_iterations(act, step)

            @block.vector
            def _(dve):
                v = nc.vector

                def finish_gcn(ch):
                    c, nj = ch.c, ch.nj
                    dve.wait_ge(s_gm, c + 1)
                    for j in range(nj):
                        v.scalar_tensor_tensor(x2[:, j, :], ps[:, 6, j * 256:(j + 1) * 256],
                                               dinv[:, bass.ds(2 * c + j, 1)], gcn_b, ALU.mult, ALU.add)
                    dve.drain()
                    dve.wait_ge(s_rl, 16 * (c + 1))
                    v.scalar_tensor_tensor(x2[:, 0:nj, :], x2[:, 0:nj, :], 0.0, res_in[:, 0:nj, :], ALU.max, ALU.add)
                    dve.drain().then_inc(s_x2, 1)
                    ge(dve, s_xnp, c)
                    src = x2
                    for _ in range(2):
                        for j in range(nj):
                            v.bn_stats(st2[:, j, :], src[:, j, :])
                        dve.drain()
                        for j in range(nj):
                            v.bn_aggr(mv2[:, j, :], st2[:, j, :])
                        dve.drain()
                        v.tensor_scalar(var2[:, 0:nj], mv2[:, 0:nj, 1], EPS, None, ALU.add)
                        dve.drain()
                        rsqrt(dve, rs2[:, 0:nj], var2[:, 0:nj], sm(166, nj))
                        for j in range(nj):
                            v.tensor_scalar(xn[:, j, :], src[:, j, :], mv2[:, j, 0:1], rs2[:, j:j + 1],
                                            ALU.subtract, ALU.mult)
                        dve.drain()
                        src = xn
                    v.nop().then_inc(s_xn, 1)

                def stage(ch):
                    v.tensor_copy(staged[:, :, 0:ch.n], aggT[:, :, bass.ds(ch.c * CH, ch.n)])
                    dve.drain().then_inc(s_st, 1)

                def add_expert(ch, e):
                    x = NE * ch.c + e
                    dve.wait_ge(s_yd, x + 1)
                    dst = y_acc if e < NE - 1 else y_out
                    if e == NE - 1:
                        ge(dve, s_ys, 16 * ch.c)
                    for j in range(ch.nj):
                        v.scalar_tensor_tensor(dst[:, j, :], ps[:, 4 + e % 2, j * 256:(j + 1) * 256],
                                               w_full[:, j, e:e + 1], y_acc[:, j, :], ALU.mult, ALU.add)
                    dve.drain().then_inc(s_ya, 1)
                    if e == NE - 1:
                        v.nop().then_inc(s_yo, 1)

                def route(ch):
                    c, nj = ch.c, ch.nj
                    dve.wait_ge(s_lg, c + 1)
                    L = logit[:, 0:nj, :]
                    v.tensor_tensor(L, ps[:, 6, 0:nj * NE].rearrange("p (j e) -> p j e", e=NE),
                                    br_bc.unsqueeze(1).to_broadcast([P, nj, NE]), ALU.add)
                    dve.drain()
                    for j in range(nj):
                        v.max(out=top[:, j, :], in_=logit[:, j, :])
                        mine = logit[:, j, :].unsqueeze(2).to_broadcast([P, NE, NE])
                        theirs = logit[:, j, :].unsqueeze(1).to_broadcast([P, NE, NE])
                        v.tensor_tensor(cmp[:, j, :, :], theirs, mine, ALU.is_gt)
                        v.tensor_tensor(cmp2[:, j, :, :], theirs, mine, ALU.is_equal)
                    dve.drain()
                    for j in range(nj):
                        v.tensor_tensor(cmp2[:, j, :, :], cmp2[:, j, :, :], before[:, :, :], ALU.mult)
                    v.tensor_tensor(gap[:, 0:nj], top[:, 0:nj, 0], top[:, 0:nj, 1], ALU.subtract)
                    if nj == 1:
                        v.memset(gap[:, 1:2], 0.0)
                    dve.drain().then_inc(s_gap, 1)
                    v.tensor_tensor(cmp[:, 0:nj, :, :].rearrange("p j e f -> p (j e f)"),
                                    cmp[:, 0:nj, :, :].rearrange("p j e f -> p (j e f)"),
                                    cmp2[:, 0:nj, :, :].rearrange("p j e f -> p (j e f)"), ALU.add)
                    dve.drain()
                    v.reduce_sum(rank[:, 0:nj, :].rearrange("p j e -> p (j e)"),
                                 cmp[:, 0:nj, :, :].rearrange("p j e f -> p (j e) f"), axis=AX_X)
                    dve.wait_ge(s_th, c + 1)
                    v.tensor_scalar(w_top[:, 0, :], gap[:, :], 0.5, 0.5, ALU.mult, ALU.add)
                    v.tensor_scalar(w_top[:, 1, :], gap[:, :], -0.5, 0.5, ALU.mult, ALU.add)
                    dve.drain()
                    for j in range(nj):
                        v.tensor_scalar(w_tmp[:, j, :], rank[:, j, :], 0.0, w_top[:, 0, j:j + 1],
                                        ALU.is_equal, ALU.mult)
                        v.tensor_scalar(w_full[:, j, :], rank[:, j, :], 1.0, w_top[:, 1, j:j + 1],
                                        ALU.is_equal, ALU.mult)
                    dve.drain()
                    v.tensor_tensor(w_full[:, 0:nj, :], w_full[:, 0:nj, :], w_tmp[:, 0:nj, :], ALU.add)
                    dve.drain().then_inc(s_wf, 1)
                    dve.wait_ge(s_wt, c + 1)
                    v.tensor_copy(wT[:, 0:ch.n], ps[0:NE, 7, 0:ch.n]).then_inc(s_wc, 1)
                    dve.wait_ge(s_yb, c + 1)
                    v.tensor_tensor(y_acc[:, 0:nj, :], x2[:, 0:nj, :], halves(ps[:, 6, :])[:, 0:nj, :], ALU.add)
                    dve.drain().then_inc(s_yb_read, 1)

                def step(it, k, agg, prev, cur):
                    if agg:
                        l2.dve(dve, it, k, isinstance(it, int) and GI * it + k == GROUPS - 1)
                    if k == 0 and prev:
                        add_expert(prev, 4)
                    if k == PRE_STEP:
                        if cur:
                            stage(cur)
                        if prev:
                            add_expert(prev, 5)
                        if cur:
                            finish_gcn(cur)
                        if prev:
                            add_expert(prev, 6)
                    if k == PRE_STEP + 1:
                        if prev:
                            add_expert(prev, 7)
                        if cur:
                            route(cur)
                    if k > PRE_STEP + 1 and cur:
                        for e in STEP_EXPERTS[k]:
                            add_expert(cur, e - 1)
                l2.make_s(dve, 0, 0)
                over_iterations(dve, step)


_INS = ["x", "src", "dst", "edge_weight", "L0_gnn_W1", "L0_gnn_b1", "L0_gnn_W2", "L0_gnn_b2",
        "L0_mix_wq", "L0_mix_bq", "L0_mix_wk", "L0_mix_bk", "L0_mix_wv", "L0_mix_bv", "L0_mix_wo", "L0_mix_bo",
        "L0_ffn_gamma", "L0_ffn_beta", "L0_ffn_Wr", "L0_ffn_br", "L0_ffn_W1", "L0_ffn_b1", "L0_ffn_W2", "L0_ffn_b2"]


def kernel(**inputs):
    import numpy as _np
    import concourse.bacc as _bacc
    from concourse import mybir as _mybir
    from concourse.bass_utils import run_bass_kernel_spmd as _run

    nc = _bacc.Bacc("TRN2", target_bir_lowering=False, num_devices=1)
    arrays, aps = {}, {}
    for name in _INS:
        a = _np.ascontiguousarray(inputs[name])
        arrays[f"in_{name}"] = a
        aps[name] = nc.dram_tensor(f"in_{name}", a.shape, _mybir.dt.from_np(a.dtype), kind="ExternalInput").ap()
    out = nc.dram_tensor("out_0", (N, D), F32, kind="ExternalOutput").ap()
    gps_layer(nc, aps, out)
    r = _run(nc, [arrays], core_ids=[0])
    return r.results[0]["out_0"]
```

```python
import concourse.bass as bass
from concourse import mybir
from contextlib import ExitStack

P = 128
F32 = mybir.dt.float32
BF16 = mybir.dt.bfloat16
I32 = mybir.dt.int32
U32 = mybir.dt.uint32
ALU = mybir.AluOpType
ACT = mybir.ActivationFunctionType
AX_X = mybir.AxisListType.X

N = 6250
D = 256
E = 206250
KH = D // P
NT = -(-N // P)
LAST = N - (NT - 1) * P
NP = 6336
EDGE_TILES = 11
HALVES = ((0, 6), (6, 11))
WIN = 32
SWIN = 64
QUARTERS = [(0, 0), (1, 1), (6, 2), (7, 3), (2, 0), (3, 1), (8, 2), (9, 3), (4, 0), (5, 1), (10, 2)]
ROWS = -(-E // P)
GROUPS = -(-ROWS // EDGE_TILES)
ET = GROUPS * EDGE_TILES
EBLK = -(-ET // P)
GI = 6
CH = 256
ITERS = GROUPS // GI
G_REST = GROUPS - ITERS * GI
CHUNKS = -(-N // CH)
PRE_STEP = 1
RING = 3
SLOW_WIN = -(-N // SWIN)
NE, H = 8, 512
HC = H // P
HEADS, DEPTH = 8, 32
EPS = 1e-5
GATHER_INC = 16 * EDGE_TILES


def ge(eng, sem, value):
    if isinstance(value, int) and value <= 0:
        return
    eng.wait_ge(sem, value)


def gps_layer(nc, A, out):
    ctx = ExitStack()
    with ctx:
        def sb(name, shape, dt=F32):
            return ctx.enter_context(nc.sbuf_tensor(name, shape, dt))

        def sem(name):
            return ctx.enter_context(nc.semaphore(name))

        z_dram = [nc.dram_tensor(f"z{i}_rows", [N, D], F32).ap() for i in (1, 2)]
        res_dram = nc.dram_tensor("residual_rows", [N, D], F32).ap()
        stray_dram = nc.dram_tensor("stray_dst", [P, ET], F32).ap()

        big = sb("big", [P, 16384])
        aggT = sb("aggT", [P, KH, NP])
        srcT = sb("srcT", [P, ET], U32)
        dstL = sb("dstL", [P, ET])
        ewT = sb("ewT", [P, ET])
        rows = sb("rows", [P, RING, EDGE_TILES, D])
        S = sb("S", [P, RING, EDGE_TILES, WIN])
        S_stray = S[:, :, :, :].rearrange("p a b c -> p (a b c)")[:, 0:EDGE_TILES * SWIN]\
            .rearrange("p (t w) -> p t w", w=SWIN)
        strips = sb("strips", [P, 2, D])
        idx = sb("idx", [P, GI, EDGE_TILES], U32)
        base_i = sb("base_i", [1, GROUPS, 4], I32)
        flag_i = sb("flag_i", [1, 1], I32)
        ident = sb("ident", [P, P])
        ones = sb("ones", [P, P])
        iota_w = sb("iota_w", [P, SWIN])
        win_start = sb("win_start", [P, SLOW_WIN])
        before = sb("before", [P, NE, NE])
        dinv = sb("dinv", [P, NT])
        stray_t = sb("stray_t", [P, EDGE_TILES])
        ps = ctx.enter_context(nc.psum_tensor("ps", [P, 8, 512], F32))

        scratch = sb("scratch", [P, 14, 512])
        small = sb("small", [P, 256])

        def piece(n, k=1):
            return scratch[:, n:n + k, :].rearrange("p a b -> p (a b)")

        def halves(v):
            return v.rearrange("p (k n) -> p k n", k=2)

        def rsqrt(dve, y, x, t):
            v = nc.vector
            v.tensor_scalar(t.bitcast(I32), x.bitcast(I32), 1, None, ALU.logical_shift_right)
            dve.drain()
            v.tensor_scalar(y.bitcast(I32), t.bitcast(I32), -1.0, float(0x5F3759DF), ALU.mult, ALU.add)
            dve.drain()
            for _ in range(3):
                v.tensor_tensor(t, y, y, ALU.mult)
                dve.drain()
                v.scalar_tensor_tensor(t, t, -0.5, x, ALU.mult, ALU.mult)
                dve.drain()
                v.scalar_tensor_tensor(y, t, 1.5, y, ALU.add, ALU.mult)
                dve.drain()

        o = EBLK * P
        row_dst_i = big[:, 0:o].bitcast(I32)
        row_src_i = big[:, o:2 * o].bitcast(I32)
        row_ew = big[:, 2 * o:3 * o]
        row_dst = big[:, 3 * o:4 * o]
        row_src = big[:, 4 * o:5 * o]
        dstT = big[:, 5 * o:5 * o + ET]
        stray = big[:, 6 * o:6 * o + ET]
        tmp_e = big[:, 7 * o:7 * o + ET]
        r0 = 8 * o
        frontier = big[:, r0:r0 + GROUPS]
        tmp_i = big[:, r0 + 256:r0 + 512].bitcast(I32)
        ew3 = rows[:, 0, :, :].rearrange("p a b -> p (a b)").bitcast(BF16)[:, 0:3 * ET]\
            .rearrange("p (t c) -> p t c", c=3)
        deg_oh = rows[:, 1, :, :].rearrange("p a b -> p (a b)").bitcast(BF16)[:, 0:3 * EDGE_TILES * SWIN]\
            .rearrange("p (s t w) -> p s t w", s=3, w=SWIN)
        FULL_BLK = EBLK - 1
        tail_row0 = FULL_BLK * P
        tail_rows = E // P - tail_row0
        tail_edges = E - (E // P) * P

        s_c = sem("const_step")
        s_pad = sem("pads_written")
        s_load = sem("edges_loaded")
        s_cast = sem("rows_cast")
        s_tr = sem("rows_transposed")
        s_ev = sem("edges_evacuated")
        s_base = sem("bases_spread")
        s_flag = sem("stray_count")
        s_flag2 = sem("stray_sum")
        s_stray = sem("strays_ready")
        s_sstore = sem("strays_stored")

        with nc.Block() as block:
            @block.sync
            def _(sp):
                for dst, src in ((row_dst_i, A["dst"]), (row_src_i, A["src"]), (row_ew, A["edge_weight"])):
                    sp.dma_start(dst[:, 0:FULL_BLK * P].rearrange("p (b c) -> p b c", c=P),
                                 src[0:FULL_BLK * P * P].rearrange("(b r c) -> r b c", r=P, c=P))\
                      .then_inc(s_load, 16)
                sp.wait_ge(s_pad, 3)
                for dst, src in ((row_dst_i, A["dst"]), (row_src_i, A["src"]), (row_ew, A["edge_weight"])):
                    e0 = tail_row0 * P
                    sp.dma_start(dst[0:tail_rows, FULL_BLK * P:EBLK * P],
                                 src[e0:e0 + tail_rows * P].rearrange("(r c) -> r c", c=P)).then_inc(s_load, 16)
                    sp.dma_start(dst[tail_rows:tail_rows + 1, FULL_BLK * P:FULL_BLK * P + tail_edges],
                                 src[e0 + tail_rows * P:E].rearrange("(r c) -> r c", r=1)).then_inc(s_load, 16)
                sp.wait_ge(s_stray, 1)
                sp.dma_start(stray_dram[:, :], dstT).then_inc(s_sstore, 16)
                sp.wait_ge(s_sstore, 16)

            @block.gpsimd
            def _(pool):
                g = nc.gpsimd
                g.memset(row_dst_i[:, FULL_BLK * P:EBLK * P], N).then_inc(s_pad, 1)
                g.memset(row_src_i[:, FULL_BLK * P:EBLK * P], 0).then_inc(s_pad, 1)
                g.memset(row_ew[:, FULL_BLK * P:EBLK * P], 0.0).then_inc(s_pad, 1)
                g.memset(ident[:, :], 0.0).then_inc(s_c, 1)
                g.memset(ones[:, :], 1.0).then_inc(s_c, 1)
                pool.wait_ge(s_c, 2)
                g.affine_select(out=ident[:, :], in_=ident[:, :], compare_op=ALU.not_equal, fill=1.0,
                                base=0, pattern=[[-1, P]], channel_multiplier=1).then_inc(s_c, 1)
                g.memset(frontier[:, 0:PRE_STEP + 1], 0.0).then_inc(s_c, 1)
                g.iota(tmp_i[:, 0:25 * GI], [[CH, 25], [0, GI]], base=0, channel_multiplier=0).then_inc(s_c, 1)
                pool.wait_ge(s_c, 5)
                g.tensor_copy(frontier[:, PRE_STEP + 1:GROUPS], tmp_i[:, 0:GROUPS - PRE_STEP - 1]).then_inc(s_c, 1)
                pool.wait_ge(s_c, 6)
                g.iota(tmp_i[:, 0:SWIN], [[1, SWIN]], base=0, channel_multiplier=0).then_inc(s_c, 1)
                pool.wait_ge(s_c, 7)
                g.tensor_copy(iota_w[:, :], tmp_i[:, 0:SWIN]).then_inc(s_c, 1)
                pool.wait_ge(s_c, 8)
                g.iota(tmp_i[:, 0:SLOW_WIN], [[SWIN, SLOW_WIN]], base=0, channel_multiplier=0).then_inc(s_c, 1)
                pool.wait_ge(s_c, 9)
                g.tensor_copy(win_start[:, :], tmp_i[:, 0:SLOW_WIN]).then_inc(s_c, 1)
                pool.wait_ge(s_c, 10)
                g.iota(tmp_i[:, 0:NE * NE], [[-1, NE], [1, NE]], base=0, channel_multiplier=0).then_inc(s_c, 1)
                pool.wait_ge(s_c, 11)
                g.tensor_copy(before[:, :, :].rearrange("p a b -> p (a b)"), tmp_i[:, 0:NE * NE]).then_inc(s_c, 1)

            @block.tensor
            def _(pe):
                pe.wait_ge(s_c, 3)
                for n, rows_f in enumerate((row_dst, row_ew, row_src)):
                    bank = 4 * (n % 2)
                    pe.wait_ge(s_cast, n + 1)
                    if n == 2:
                        pe.wait_ge(s_ev, 1)
                    for b in range(EBLK):
                        m = P if b < FULL_BLK else ET - FULL_BLK * P
                        mm = nc.tensor.transpose(ps[:, bank + b // 4, (b % 4) * P:(b % 4) * P + m],
                                                 rows_f[0:m, b * P:(b + 1) * P], ident[0:m, 0:m])
                    mm.then_inc(s_tr, 1)
                pe.wait_ge(s_ev, 3)
                first = dstT.rearrange("p (g t) -> p g t", t=EDGE_TILES)
                for h, (t0, _) in enumerate(HALVES):
                    mm = nc.tensor.matmul(ps[:, 6, h * 256:h * 256 + GROUPS], ones[0:1, :], first[0:1, :, t0],
                                          start=True, stop=True)
                mm.then_inc(s_base, 1)
                pe.wait_ge(s_flag, 1)
                nc.tensor.matmul(ps[0:1, 7, 0:1], ones[:, 0:1], small[:, 0:1], start=True, stop=True)\
                  .then_inc(s_flag2, 1)

            @block.vector
            def _(dve):
                v = nc.vector
                v.memset(aggT[:, :, :], 0.0)
                v.memset(small[:, :], 0.0)
                v.memset(base_i[:, :, 2:4], 0)
                dve.wait_ge(s_load, 16 * 9)
                v.tensor_copy(row_dst, row_dst_i).then_inc(s_cast, 2)
                v.tensor_copy(row_src, row_src_i).then_inc(s_cast, 1)
                for n, dst in enumerate((dstT, ewT[:, :], srcT[:, :])):
                    dve.wait_ge(s_tr, n + 1)
                    bank = 4 * (n % 2)
                    v.tensor_copy(dst, ps[:, bank:bank + 4, :].rearrange("p a b -> p (a b)")[:, 0:ET])\
                     .then_inc(s_ev, 1)
                dve.wait_ge(s_ev, 3)
                grp = lambda a: a.rearrange("p (g t) -> p g t", t=EDGE_TILES)
                for h, (t0, _) in enumerate(HALVES):
                    v.tensor_copy(base_i[0:1, :, h], grp(dstT)[0:1, :, t0])
                dve.wait_ge(s_base, 1)
                dve.wait_ge(s_c, 12)
                for h, (t0, t1) in enumerate(HALVES):
                    v.tensor_tensor(grp(dstL[:, :])[:, :, t0:t1], grp(dstT)[:, :, t0:t1],
                                    ps[:, 6, h * 256:h * 256 + GROUPS].unsqueeze(2)
                                    .to_broadcast([P, GROUPS, t1 - t0]), ALU.subtract)
                v.tensor_tensor(grp(stray), grp(dstT),
                                frontier.unsqueeze(2).to_broadcast([P, GROUPS, EDGE_TILES]), ALU.is_lt)
                dve.drain()
                v.scalar_tensor_tensor(tmp_e, dstL[:, :], 0.0, stray, ALU.is_lt, ALU.max)
                dve.drain()
                v.scalar_tensor_tensor(stray, dstL[:, :], float(WIN) - 0.5, tmp_e, ALU.is_gt, ALU.max)
                dve.drain()
                v.reduce_sum(small[:, 0:1], stray, axis=AX_X).then_inc(s_flag, 1)
                v.scalar_tensor_tensor(dstL[:, :], stray, -20000.0, dstL[:, :], ALU.mult, ALU.add)
                v.scalar_tensor_tensor(tmp_e, dstT, 1.0, stray, ALU.add, ALU.mult)
                v.tensor_copy(ew3[:, :, 0], ewT[:, :])
                dve.drain()
                v.tensor_scalar(dstT, tmp_e, -1.0, None, ALU.add).then_inc(s_stray, 1)
                v.tensor_tensor(stray, ewT[:, :], ew3[:, :, 0], ALU.subtract)
                dve.drain()
                v.tensor_copy(ew3[:, :, 1], stray)
                dve.drain()
                v.tensor_tensor(tmp_e, stray, ew3[:, :, 1], ALU.subtract)
                dve.drain()
                v.tensor_copy(ew3[:, :, 2], tmp_e)
                v.tensor_scalar(before[:, :, :], before[:, :, :], 0.0, None, ALU.is_lt)
                dve.wait_ge(s_flag2, 1)
                v.tensor_copy(flag_i[0:1, 0:1], ps[0:1, 7, 0:1])

        deg3 = big[0:3, 0:NP]
        stray_dst = rows[:, 2, :, :].rearrange("p a b -> p (a b)")[:, 0:ET]
        DG = 3
        s_oh = sem("onehot_ready")
        s_dm = sem("degree_summed")
        s_e3 = sem("weight_parts_staged")
        s_da = sem("degree_added")
        s_dmc = sem("degree_transposed")
        s_slq = sem("slow_strays_loaded")
        s_soh = sem("slow_onehot_ready")
        s_sdm = sem("slow_degree_summed")

        def iota_b(w):
            return iota_w[:, 0:w].unsqueeze(1).to_broadcast([P, EDGE_TILES, w])

        ew3s = small[:, 0:DG * 3 * EDGE_TILES // 2 + 1].bitcast(BF16)[:, 0:DG * 3 * EDGE_TILES]\
            .rearrange("p (s t c) -> p s t c", s=DG, c=3)

        def bases(g, n=1):
            k = 2 if n == 1 else 4
            _, values = nc.values_load_multi_w_load_instructions(
                base_i[0:1, bass.ds(g, n), 0:k].rearrange("a g h -> a (g h)") if n > 1
                else base_i[0:1, bass.ds(g, 1), 0:k].rearrange("a g h -> a (g h)"),
                engines=[mybir.EngineType.DVE], min_val=0, max_val=N)
            return values

        def local(a, g, w=WIN):
            return a[:, bass.ds(g * EDGE_TILES, EDGE_TILES)].unsqueeze(2).to_broadcast([P, EDGE_TILES, w])

        with nc.Block() as block:
            @block.gpsimd
            def _(pool):
                def parts(i, k):
                    g = DG * i + k
                    ge(pool, s_dm, g - DG + 1)
                    nc.gpsimd.tensor_copy(ew3s[:, k, :, :], ew3[:, bass.ds(g * EDGE_TILES, EDGE_TILES), :])\
                      .then_inc(s_e3, 1)
                for k in range(DG):
                    parts(0, k)
                with pool.Fori(1, GROUPS // DG) as i:
                    for k in range(DG):
                        parts(i, k)

            @block.tensor
            def _(pe):
                def group(i, k):
                    g = DG * i + k
                    pe.wait_ge(s_e3, g + 1)
                    pe.wait_ge(s_oh, g + 1)
                    ge(pe, s_da, g - DG + 1)
                    for h, (t0, t1) in enumerate(HALVES):
                        for t in range(t0, t1):
                            mm = nc.tensor.matmul(ps[0:3, k, h * WIN:(h + 1) * WIN], ew3s[:, k, t, :],
                                                  deg_oh[:, k, t, 0:WIN], start=(t == t0), stop=(t == t1 - 1))
                    mm.then_inc(s_dm, 1)
                for k in range(DG):
                    group(0, k)
                with pe.Fori(1, GROUPS // DG) as i:
                    for k in range(DG):
                        group(i, k)

            @block.vector
            def _(dve):
                v = nc.vector
                v.memset(deg3, 0.0)

                def onehot(i, k):
                    g = DG * i + k
                    ge(dve, s_dm, g - DG + 1)
                    v.tensor_tensor(deg_oh[:, k, :, 0:WIN], local(dstL, g), iota_b(WIN), ALU.is_equal)\
                     .then_inc(s_oh, 1)

                def add(i, k, b):
                    g = DG * i + k
                    dve.wait_ge(s_dm, g + 1)
                    for h in range(2):
                        at = deg3[:, bass.ds(b[4 * k + h], WIN)]
                        v.tensor_tensor(at, at, ps[0:3, k, h * WIN:(h + 1) * WIN], ALU.add)
                        last = dve.drain()
                    last.then_inc(s_da, 1)

                dve.drain()
                for k in range(DG):
                    onehot(0, k)
                with dve.Fori(0, GROUPS // DG - 1) as i:
                    b = bases(DG * i, DG)
                    for k in range(DG):
                        add(i, k, b)
                        onehot(i + 1, k)
                b = bases(GROUPS - DG, DG)
                for k in range(DG):
                    add(GROUPS // DG - 1, k, b)

        with nc.Block() as block:
            @block.sync
            def _(sp):
                f = sp.value_load(flag_i[0:1, 0:1], min_val=0, max_val=ET * P)
                with sp.If(f != 0):
                    sp.dma_start(stray_dst, stray_dram[:, :]).then_inc(s_slq, 16)
                    sp.wait_ge(s_slq, 16)
                sp.nop()

            @block.tensor
            def _(pe):
                f = pe.value_load(flag_i[0:1, 0:1], min_val=0, max_val=ET * P)
                with pe.If(f != 0):
                    with pe.Fori(0, GROUPS) as g:
                        with pe.Fori(0, SLOW_WIN) as w:
                            pe.wait_ge(s_soh, SLOW_WIN * g + w + 1)
                            for t in range(EDGE_TILES):
                                mm = nc.tensor.matmul(ps[0:3, 0, 0:SWIN], ew3s[:, 0, t, :], deg_oh[:, 0, t, :],
                                                      start=(t == 0), stop=(t == EDGE_TILES - 1))
                            mm.then_inc(s_sdm, 1)
                pe.nop()

            @block.vector
            def _(dve):
                v = nc.vector
                f = dve.value_load(flag_i[0:1, 0:1], min_val=0, max_val=ET * P)
                with dve.If(f != 0):
                    dve.wait_ge(s_slq, 16)
                    with dve.Fori(0, GROUPS) as g:
                        with dve.Fori(0, SLOW_WIN) as w:
                            v.tensor_copy(ew3s[:, 0, :, :], ew3[:, bass.ds(g * EDGE_TILES, EDGE_TILES), :])
                            v.tensor_scalar(stray_t[:, :], stray_dst[:, bass.ds(g * EDGE_TILES, EDGE_TILES)],
                                            win_start[:, bass.ds(w, 1)], None, ALU.subtract)
                            dve.drain()
                            v.tensor_tensor(deg_oh[:, 0, :, :], stray_t[:, :].unsqueeze(2)
                                            .to_broadcast([P, EDGE_TILES, SWIN]), iota_b(SWIN), ALU.is_equal)
                            dve.drain().then_inc(s_soh, 1)
                            dve.wait_ge(s_sdm, SLOW_WIN * g + w + 1)
                            v.tensor_tensor(deg3[:, bass.ds(w * SWIN, SWIN)], deg3[:, bass.ds(w * SWIN, SWIN)],
                                            ps[0:3, 0, 0:SWIN], ALU.add)
                            dve.drain()
                dve.nop()

        s_dn = sem("degrees_by_node")
        dtmp = small[:, 0:NT]
        dpos = small[:, 64:64 + NT]
        with nc.Block() as block:
            @block.tensor
            def _(pe):
                for j in range(NT):
                    mm = nc.tensor.matmul(ps[:, 0, j:j + 1], deg3[:, j * P:(j + 1) * P], ones[0:3, 0:1],
                                          start=True, stop=True)
                mm.then_inc(s_dn, 1)

            @block.vector
            def _(dve):
                v = nc.vector
                dve.wait_ge(s_dn, 1)
                v.tensor_scalar(dtmp, ps[:, 0, 0:NT], 1.0, 1e-30, ALU.add, ALU.max)
                v.tensor_scalar(dpos, ps[:, 0, 0:NT], 1.0, 0.0, ALU.add, ALU.is_gt)
                dve.drain()
                rsqrt(dve, dinv[:, :], dtmp, small[:, 128:128 + NT])
                v.tensor_tensor(dinv[:, :], dinv[:, :], dpos, ALU.mult)

        XK = 4
        xT = big[:, 0:KH * NT * P].rearrange("p (k n) -> p k n", k=KH)
        o = KH * NT * P
        wkv = big[:, o:o + 1024].rearrange("p (k n) -> p k n", k=KH)
        wq = big[:, o + 1024:o + 1536].rearrange("p (k n) -> p k n", k=KH)
        wo = big[:, o + 1536:o + 2048].rearrange("p (k n) -> p k n", k=KH)
        kv_bd = big[:, o + 2048:o + 2304].rearrange("p (k n) -> p k n", k=KH)
        ks_bd = big[:, o + 2304:o + 2560].rearrange("p (k n) -> p k n", k=KH)
        blockdiag = big[:, o + 2560:o + 2560 + P]
        bias_kv = big[:, o + 2688:o + 2688 + 512]
        bq_col = big[:, o + 3200:o + 3202]
        bo_bc = big[:, o + 3204:o + 3204 + D]

        def pool_ring(n):
            return rows[:, n // 2, :, :].rearrange("p a b -> p (a b)")[:, (n % 2) * 1024:(n % 2 + 1) * 1024]\
                .rearrange("p (s d) -> p s d", s=XK)
        x_in, x_hat, z_row = (pool_ring(n) for n in range(3))
        kv_raw = piece(2)
        k_neg, k_feat = piece(3)[:, 0:D], piece(3)[:, D:2 * D]
        v_one = piece(4)[:, 0:2 * 129]
        x_tile = halves(piece(5))[:, :, 0:P]
        stats = small[:, 0:XK * 6].rearrange("p (s c) -> p s c", s=XK)
        mv = small[:, 32:32 + XK * 2].rearrange("p (s c) -> p s c", s=XK)
        rstd = small[:, 48:48 + XK]
        var = small[:, 52:52 + XK]

        s_w = sem("mix_weights_loaded")
        s_bd = sem("mix_constants")
        s_xl = [sem(f"x_loaded{s}") for s in range(XK)]
        s_xh = sem("x_hat_ready")
        s_z = sem("z_ready")
        s_zs = [sem(f"z_stored{s}") for s in range(XK)]
        s_xt = sem("tiles_transposed")
        s_xe = sem("transposes_evacuated")
        def row_bc(v):
            return v.rearrange("(a n) -> a n", a=1).to_broadcast([P, v.shape[0]])

        x_tiles = A["x"]

        with nc.Block() as block:
            @block.sync
            def _(sp):
                for w, n0 in (("L0_mix_wk", 0), ("L0_mix_wv", D)):
                    sp.dma_start(wkv[:, :, n0:n0 + D], A[w].rearrange("(k p) n -> p k n", p=P)).then_inc(s_w, 16)
                sp.dma_start(bias_kv[:, 0:D], row_bc(A["L0_mix_bk"])).then_inc(s_w, 16)
                sp.dma_start(bias_kv[:, D:2 * D], row_bc(A["L0_mix_bv"])).then_inc(s_w, 16)
                sp.dma_start(wq, A["L0_mix_wq"].rearrange("(k p) n -> p k n", p=P)).then_inc(s_w, 16)
                sp.dma_start(wo, A["L0_mix_wo"].rearrange("(k p) n -> p k n", p=P)).then_inc(s_w, 16)
                sp.dma_start(bo_bc, row_bc(A["L0_mix_bo"])).then_inc(s_w, 16)
                with nc.allow_non_contiguous_dma(reason="256 biases, one per partition"):
                    sp.dma_start(bq_col, A["L0_mix_bq"].rearrange("(k p) -> p k", p=P)).then_inc(s_w, 16)

                def load(i, k, n):
                    ge(sp, s_xh, XK * (i - 1) + k + 1 if not isinstance(i, int) or i > 0 else 0)
                    sp.dma_start(x_in[0:n, k, :], x_tiles[bass.ds((XK * i + k) * P, n), :]).then_inc(s_xl[k], 16)
                for k in range(XK):
                    load(0, k, P)
                with sp.Fori(1, NT // XK) as i:
                    for k in range(XK):
                        load(i, k, P)
                load(NT // XK, 0, LAST)

            @block.gpsimd
            def _(pool):
                g = nc.gpsimd
                g.memset(blockdiag, 0.0).then_inc(s_bd, 1)
                g.memset(v_one, 1.0).then_inc(s_bd, 1)
                for h in range(P // DEPTH):
                    r = slice(h * DEPTH, (h + 1) * DEPTH)
                    pool.wait_ge(s_bd, 2 + h)
                    g.memset(blockdiag[r, r], 1.0).then_inc(s_bd, 1)

            @block.scalar
            def _(act):
                a = nc.scalar

                def store_z(i, k, n):
                    j = XK * i + k
                    act.wait_ge(s_z, j + 1)
                    act.dma_start(z_dram[0][bass.ds(j * P, n), :], z_row[0:n, k, :]).then_inc(s_zs[k], 16)

                def evac(i, k, n):
                    j = XK * i + k
                    act.wait_ge(s_xt, j + 1)
                    a.activation(xT[:, :, bass.ds(j * P, n)],
                                 ps[:, k % 2, 0:256].rearrange("p (k n) -> p k n", k=KH)[:, :, 0:n], ACT.Copy)
                    a.activation(aggT[:, :, bass.ds(j * P, n)],
                                 ps[:, k % 2, 256:512].rearrange("p (k n) -> p k n", k=KH)[:, :, 0:n], ACT.Copy)\
                     .then_inc(s_xe, 1)

                def tiles(i, ks, n):
                    for k in ks:
                        store_z(i, k, n)
                        evac(i, k, n)
                tiles(0, range(XK), P)
                with act.Fori(1, NT // XK) as i:
                    tiles(i, range(XK), P)
                tiles(NT // XK, range(1), LAST)
                for k in range(XK):
                    act.wait_ge(s_zs[k], 16 * (NT // XK + (k == 0)))

            @block.vector
            def _(dve):
                v = nc.vector

                def norm(i, ks, n):
                    for k in ks:
                        dve.wait_ge(s_xl[k], 16 * (i + 1))
                        v.bn_stats(stats[0:n, k, :], x_in[0:n, k, :])
                    dve.drain()
                    for k in ks:
                        v.bn_aggr(mv[0:n, k, :], stats[0:n, k, :])
                    dve.drain()
                    v.tensor_scalar(var[0:n, 0:len(ks)], mv[0:n, 0:len(ks), 1], EPS, None, ALU.add)
                    dve.drain()
                    rsqrt(dve, rstd[0:n, 0:len(ks)], var[0:n, 0:len(ks)], small[0:n, 56:56 + len(ks)])
                    for k in ks:
                        j = XK * i + k
                        ge(dve, s_xt, j - XK + 1)
                        v.tensor_scalar(x_hat[0:n, k, :], x_in[0:n, k, :], mv[0:n, k, 0:1], rstd[0:n, k:k + 1],
                                        ALU.subtract, ALU.mult).then_inc(s_xh, 1)
                    dve.drain()
                    for k in ks:
                        ge(dve, s_zs[k], 16 * i)
                        v.tensor_scalar(z_row[0:n, k, :], x_hat[0:n, k, :], dinv[0:n, bass.ds(XK * i + k, 1)],
                                        None, ALU.mult).then_inc(s_z, 1)

                norm(0, range(XK), P)
                with dve.Fori(1, NT // XK) as i:
                    norm(i, range(XK), P)
                norm(NT // XK, range(1), LAST)

            @block.tensor
            def _(pe):
                t = nc.tensor

                def trans(i, k, n):
                    j = XK * i + k
                    pe.wait_ge(s_z, j + 1)
                    ge(pe, s_xe, j - 1)
                    for m, src in enumerate((x_hat, z_row)):
                        for h in range(KH):
                            mm = t.transpose(ps[:, k % 2, m * 256 + h * P:m * 256 + h * P + n],
                                             src[0:n, k, h * P:(h + 1) * P], ident[0:n, 0:n])
                    mm.then_inc(s_xt, 1)

                def tiles(i, ks, n):
                    for k in ks:
                        trans(i, k, n)
                tiles(0, range(XK), P)
                with pe.Fori(1, NT // XK) as i:
                    tiles(i, range(XK), P)
                tiles(NT // XK, range(1), LAST)

        KV_STEPS = (0, 2, 3, 4, 5)
        KV_ITERS = NT // len(KV_STEPS) + 1
        Q_IT = KV_ITERS + 1
        Q_END = Q_IT + (CHUNKS - 1) // 2
        assert KV_ITERS * len(KV_STEPS) > NT and Q_END <= ITERS and GI == 6

        s_kx = sem("x_T_tile_staged")
        s_kv = sem("kv_projected")
        s_kr = sem("kv_raw_ready")
        s_ke = sem("k_exp_ready")
        s_kf = sem("k_feature_ready")
        s_ka = sem("kv_accumulated")
        s_bdr = sem("kv_blocks_ready")
        s_q = sem("q_projected")
        s_qm = sem("q_min_ready")
        s_qx = sem("q_exp_ready")
        s_qf = sem("q_feature_ready")
        s_o = sem("attention_done")
        s_on = sem("attention_normalised")
        s_m = sem("mix_projected")
        s_r = sem("residual_ready")
        s_rx = [sem(f"x_reloaded{k}") for k in range(2)]
        s_rs = [sem(f"residual_stored{k}") for k in range(2)]
        q_neg, q_pos, q_feat, o_norm, o_T = (halves(piece(n)) for n in range(2, 7))
        x_again = [halves(piece(7 + k)) for k in range(2)]
        res_out = [halves(piece(12 + k)) for k in range(2)]

        def mix_work(it, lo, k):
            if lo < KV_ITERS:
                if k not in KV_STEPS:
                    return []
                n = len(KV_STEPS) * it + KV_STEPS.index(k)
                return [] if isinstance(n, int) and n > NT else [("kv", n, 0, 0)]
            if lo < Q_IT:
                kind = {0: "spread", 2: "q1", 3: "q2", 4: "q3"}.get(k)
                return [(kind, 0, 0, 0)] if kind else []
            if lo < Q_END:
                i = it - Q_IT
                odd, even = (2 * i + 1, 1, i), (2 * i + 2, 0, i + 1)
                return {0: [("q1", *odd)], 2: [("q2", *odd)], 3: [("q3", *odd), ("q1", *even)],
                        4: [("q2", *even)], 5: [("q3", *even)]}.get(k, [])
            return []

        def tile_rows(n):
            return LAST if isinstance(n, int) and n == NT - 1 else P

        def is_number(n, value):
            return isinstance(n, int) and n == value

        def q_size(n):
            return LAST if is_number(n, 0) else CH

        def q_rows(n):
            return ((CHUNKS - 1) * CH, LAST, 1) if is_number(n, 0) else ((n - 1) * CH, P, 2)

        def mix_pe(pe, kind, n, slot, uses):
            t = nc.tensor
            if kind == "kv":
                if not is_number(n, 0):
                    m = tile_rows(n - 1)
                    pe.wait_ge(s_kf, n)
                    for a in range(KH):
                        mm = t.matmul(ps[:, 3 + a, 0:129], k_feat[0:m, a * P:(a + 1) * P],
                                      v_one[0:m, a * 129:(a + 1) * 129], start=is_number(n, 1),
                                      stop=is_number(n, NT), skip_group_check=True)
                    mm.then_inc(s_ka, 1)
                if not is_number(n, NT):
                    m = tile_rows(n)
                    pe.wait_ge(s_kx, n + 1)
                    ge(pe, s_kf, n)
                    for h in range(KH):
                        mm = t.matmul(ps[0:m, 2, :], x_tile[:, h, 0:m], wkv[:, h, :], start=(h == 0),
                                      stop=(h == KH - 1))
                    mm.then_inc(s_kv, 1)
            elif kind == "q1":
                c0, size = q_rows(n)[0], q_size(n)
                ge(pe, s_qm, n)
                for a in range(KH):
                    for h in range(KH):
                        mm = t.matmul(ps[:, 2, a * 256:a * 256 + size], wq[:, h, a * P:(a + 1) * P],
                                      xT[:, h, bass.ds(c0, size)], start=(h == 0), stop=(h == KH - 1))
                mm.then_inc(s_q, 1)
            elif kind == "q2":
                size = q_size(n)
                pe.wait_ge(s_qf, n + 1)
                pe.wait_ge(s_bdr, 1)
                ge(pe, s_on, n)
                for bank, w in ((3, kv_bd), (4, ks_bd)):
                    for a in range(KH):
                        mm = t.matmul(ps[:, bank, a * 256:a * 256 + size], w[:, a, :], q_feat[:, a, 0:size],
                                      start=True, stop=True)
                mm.then_inc(s_o, 1)
            elif kind == "q3":
                _, m, nj = q_rows(n)
                pe.wait_ge(s_on, n + 1)
                ge(pe, s_r, n)
                for j in range(nj):
                    for a in range(KH):
                        mm = t.matmul(ps[0:m, 5, j * 256:(j + 1) * 256], o_T[:, a, j * P:j * P + m], wo[:, a, :],
                                      start=(a == 0), stop=(a == KH - 1))
                mm.then_inc(s_m, 1)

        def mix_act_tile(n):
            m = tile_rows(n)
            nc.scalar.copy(x_tile[:, :, 0:m], xT[:, :, bass.ds(n * P, m)]).then_inc(s_kx, 1)

        def mix_act(act, kind, n, slot, uses):
            if kind == "kv" and not is_number(n, NT):
                m = tile_rows(n)
                act.wait_ge(s_kr, n + 1)
                nc.scalar.activation(k_neg[0:m, :], k_neg[0:m, :], ACT.Exp).then_inc(s_ke, 1)
                if not is_number(n, NT - 1):
                    mix_act_tile(n + 1)
            elif kind == "q1":
                size = q_size(n)
                act.wait_ge(s_qm, n + 1)
                nc.scalar.activation(q_neg[:, :, 0:size], q_neg[:, :, 0:size], ACT.Exp).then_inc(s_qx, 1)

        def mix_dve_first(dve, kind, n, slot, uses):
            v = nc.vector
            if kind == "kv" and not is_number(n, NT):
                m = tile_rows(n)
                dve.wait_ge(s_kv, n + 1)
                ge(dve, s_ka, n)
                v.tensor_tensor(kv_raw[0:m, :], ps[0:m, 2, :], bias_kv[0:m, :], ALU.add)
                dve.drain()
                v.tensor_scalar(k_neg[0:m, :], kv_raw[0:m, 0:D], 0.0, None, ALU.min).then_inc(s_kr, 1)
                v.tensor_copy(v_one[0:m, :].rearrange("p (k m) -> p k m", k=KH)[:, :, 0:P],
                              kv_raw[0:m, D:2 * D].rearrange("p (k m) -> p k m", k=KH))
            elif kind == "spread":
                dve.wait_ge(s_ka, NT)
                for a in range(KH):
                    v.tensor_tensor(kv_bd[:, a, :], ps[:, 3 + a, 0:P], blockdiag, ALU.mult)
                    v.tensor_copy(small[:, 64 + a:65 + a], ps[:, 3 + a, P:P + 1])
                dve.drain()
                for a in range(KH):
                    v.tensor_scalar(ks_bd[:, a, :], blockdiag, small[:, 64 + a:65 + a], None, ALU.mult)
                dve.drain().then_inc(s_bdr, 1)
            elif kind == "q1":
                size = q_size(n)
                dve.wait_ge(s_q, n + 1)
                for a in range(KH):
                    src = ps[:, 2, a * 256:a * 256 + size]
                    v.tensor_scalar(q_pos[:, a, 0:size], src, bq_col[:, a:a + 1], 0.0, ALU.add, ALU.max)
                    mn = v.tensor_scalar(q_neg[:, a, 0:size], src, bq_col[:, a:a + 1], 0.0, ALU.add, ALU.min)
                mn.then_inc(s_qm, 1)

        def mix_dve_second(dve, kind, n, slot, uses):
            v = nc.vector
            if kind == "kv" and not is_number(n, NT):
                m = tile_rows(n)
                dve.wait_ge(s_ke, n + 1)
                v.scalar_tensor_tensor(k_feat[0:m, :], kv_raw[0:m, 0:D], 0.0, k_neg[0:m, :], ALU.max, ALU.add)
                dve.drain().then_inc(s_kf, 1)
            elif kind == "q1":
                size = q_size(n)
                dve.wait_ge(s_qx, n + 1)
                v.tensor_tensor(q_feat[:, :, 0:size], q_pos[:, :, 0:size], q_neg[:, :, 0:size], ALU.add)\
                 .then_inc(s_qf, 1)
            elif kind == "q2":
                size = q_size(n)
                two = lambda bank: halves(ps[:, bank, :])[:, :, 0:size]
                dve.wait_ge(s_o, n + 1)
                v.tensor_scalar(o_norm[:, :, 0:size], two(4), 1e-6, None, ALU.add)
                dve.drain()
                v.reciprocal(o_norm[:, :, 0:size], o_norm[:, :, 0:size])
                dve.drain()
                v.tensor_tensor(o_T[:, :, 0:size], two(3), o_norm[:, :, 0:size], ALU.mult).then_inc(s_on, 1)
            elif kind == "q3":
                _, m, nj = q_rows(n)
                b = slot
                dve.wait_ge(s_rx[b], 16 * (uses + 1))
                ge(dve, s_rs[b], 16 * (uses + b))
                dve.wait_ge(s_m, n + 1)
                v.tensor_tensor(res_out[b][0:m, 0:nj, :], halves(ps[0:m, 5, :])[:, 0:nj, :],
                                x_again[b][0:m, 0:nj, :], ALU.add)
                dve.drain()
                v.tensor_tensor(res_out[b][0:m, 0:nj, :], res_out[b][0:m, 0:nj, :],
                                bo_bc[0:m, :].unsqueeze(1).to_broadcast([m, nj, D]), ALU.add).then_inc(s_r, 1)

        def stray_path(layer):
            s_l = sem(f"strays_loaded{layer}")
            s_i = sem(f"stray_idx_staged{layer}")
            s_b = sem(f"stray_gathers_begun{layer}")
            s_g = sem(f"stray_rows_gathered{layer}")
            s_s = sem(f"stray_S_ready{layer}")
            s_mm = sem(f"stray_summed{layer}")
            s_f = sem(f"stray_rows_free{layer}")
            with nc.Block() as block:
                @block.sync
                def _(sp):
                    f = sp.value_load(flag_i[0:1, 0:1], min_val=0, max_val=ET * P)
                    with sp.If(f != 0):
                        sp.dma_start(stray_dst, stray_dram[:, :]).then_inc(s_l, 16)
                        sp.wait_ge(s_l, 16)
                    sp.nop()

                @block.gpsimd
                def _(pool):
                    f = pool.value_load(flag_i[0:1, 0:1], min_val=0, max_val=ET * P)
                    with pool.If(f != 0):
                        with pool.Fori(0, GROUPS) as g:
                            pool.wait_ge(s_f, g + 1)
                            nc.gpsimd.tensor_copy(idx[:, 0, :], srcT[:, bass.ds(g * EDGE_TILES, EDGE_TILES)])\
                              .then_inc(s_i, 1)
                            pool.wait_ge(s_i, g + 1)
                            pool.sem_inc(s_b, 1)
                            for t in range(EDGE_TILES):
                                pool.indirect_dma_start(
                                    out=rows[:, 0, t, :], out_offset=None, in_=z_dram[layer][:, :],
                                    in_offset=bass.IndirectOffsetOnAxis(ap=idx[:, 0, t:t + 1], axis=0))\
                                    .then_inc(s_g, 16)
                    pool.nop()

                @block.tensor
                def _(pe):
                    f = pe.value_load(flag_i[0:1, 0:1], min_val=0, max_val=ET * P)
                    with pe.If(f != 0):
                        with pe.Fori(0, GROUPS) as g:
                            with pe.Fori(0, SLOW_WIN) as w:
                                pe.wait_ge(s_g, GATHER_INC * (g + 1))
                                pe.wait_ge(s_s, SLOW_WIN * g + w + 1)
                                for h in range(KH):
                                    for t in range(EDGE_TILES):
                                        mm = nc.tensor.matmul(ps[:, 0, h * SWIN:(h + 1) * SWIN],
                                                              rows[:, 0, t, h * P:(h + 1) * P], S_stray[:, t, :],
                                                              start=(t == 0), stop=(t == EDGE_TILES - 1))
                                mm.then_inc(s_mm, 1)
                    pe.nop()

                @block.vector
                def _(dve):
                    v = nc.vector
                    f = dve.value_load(flag_i[0:1, 0:1], min_val=0, max_val=ET * P)
                    with dve.If(f != 0):
                        dve.wait_ge(s_l, 16)
                        with dve.Fori(0, GROUPS) as g:
                            dve.sem_inc(s_f, 1)
                            with dve.Fori(0, SLOW_WIN) as w:
                                v.tensor_scalar(stray_t[:, :], stray_dst[:, bass.ds(g * EDGE_TILES, EDGE_TILES)],
                                                win_start[:, bass.ds(w, 1)], None, ALU.subtract)
                                dve.drain()
                                v.tensor_tensor(S_stray, stray_t[:, :].unsqueeze(2)
                                                .to_broadcast([P, EDGE_TILES, SWIN]), iota_b(SWIN), ALU.is_equal)
                                dve.drain()
                                v.tensor_tensor(S_stray, S_stray, local(ewT, g, SWIN), ALU.mult)\
                                 .then_inc(s_s, 1)
                                dve.wait_ge(s_mm, SLOW_WIN * g + w + 1)
                                v.tensor_tensor(aggT[:, :, bass.ds(w * SWIN, SWIN)],
                                                aggT[:, :, bass.ds(w * SWIN, SWIN)],
                                                ps[:, 0, 0:KH * SWIN].rearrange("p (k w) -> p k w", k=KH), ALU.add)
                                dve.drain()
                    dve.nop()

        class Agg:

            def __init__(self, layer):
                self.z = z_dram[layer]
                self.staged = sem(f"idx_staged{layer}")
                self.begun = sem(f"gathers_begun{layer}")
                self.gathered = [sem(f"rows_gathered{layer}_{s}") for s in range(RING)]
                self.s_ready = sem(f"S_ready{layer}")
                self.done = sem(f"group_summed{layer}")
                self.out = sem(f"sums_out{layer}")
                self.turned = sem(f"sums_transposed{layer}")
                self.added = sem(f"group_added{layer}")

            def pool(self, pool, it, k):
                g, s = GI * it + k, k % RING
                ge(pool, self.done, g - RING + 1)
                pool.wait_ge(self.staged, g + 1)
                pool.sem_inc(self.begun, 1)
                for t in range(EDGE_TILES):
                    pool.indirect_dma_start(out=rows[:, s, t, :], out_offset=None, in_=self.z[:, :],
                                            in_offset=bass.IndirectOffsetOnAxis(ap=idx[:, k, t:t + 1], axis=0))\
                        .then_inc(self.gathered[s], 16)

            def pool_all(self, pool):
                for k in range(GI):
                    self.pool(pool, 0, k)
                with pool.Fori(1, ITERS) as it:
                    for k in range(GI):
                        self.pool(pool, it, k)
                for k in range(G_REST):
                    self.pool(pool, ITERS, k)

            def stage_idx(self, it, k):
                g = GI * it + k
                nc.scalar.copy(idx[:, k % GI, :], srcT[:, bass.ds(g * EDGE_TILES, EDGE_TILES)])\
                  .then_inc(self.staged, 1)

            def act_first(self):
                for k in range(RING):
                    self.stage_idx(0, k)

            def act(self, act, it, k):
                g, b = GI * it + k, k % 2
                act.wait_ge(self.done, g + 1)
                ge(act, self.turned, g - 1)
                nc.scalar.copy(strips[:, b, :], ps[:, b, 0:D]).then_inc(self.out, 1)
                if not isinstance(it, int) or g + RING < GROUPS:
                    self.stage_idx(it, k + RING)

            def pe(self, pe, it, k):
                g, s, b = GI * it + k, k % RING, k % 2
                pe.wait_ge(self.s_ready, g + 1)
                ge(pe, self.added, g - 1)
                pe.wait_ge(self.gathered[s], GATHER_INC * (GI // RING * it + k // RING + 1))
                seen = [0] * 4
                for t, j in QUARTERS:
                    n = sum(1 for _, q in QUARTERS if q == j)
                    mm = nc.tensor.matmul(ps[j * WIN:(j + 1) * WIN, b, 0:D], S[:, s, t, :], rows[:, s, t, :],
                                          start=(seen[j] == 0), stop=(seen[j] == n - 1),
                                          tile_position=(0, j * WIN))
                    seen[j] += 1
                mm.then_inc(self.done, 1)

            def pe_turn(self, pe, it, k):
                g, b = GI * it + k, k % 2
                pe.wait_ge(self.out, g + 1)
                for h in range(KH):
                    mm = nc.tensor.transpose(ps[:, b, D + h * P:D + (h + 1) * P], strips[:, b, h * P:(h + 1) * P],
                                             ident[:, :])
                mm.then_inc(self.turned, 1)

            def make_s(self, dve, it, k):
                g, s = GI * it + k, k % RING
                ge(dve, self.done, g - RING + 1)
                nc.vector.tensor_tensor(S[:, s, :, :], local(dstL, g), iota_b(WIN), ALU.is_equal)
                dve.drain()
                nc.vector.tensor_tensor(S[:, s, :, :], S[:, s, :, :], local(ewT, g), ALU.mult)\
                  .then_inc(self.s_ready, 1)

            def add(self, dve, it, k):
                g, b = GI * it + k, k % 2
                base = bases(g)
                dve.wait_ge(self.turned, g + 1)
                strip = ps[:, b, D:2 * D].rearrange("p (k j w) -> p k j w", k=KH, w=WIN)
                for j in range(4):
                    at = aggT[:, :, bass.ds(base[j // 2], WIN)]
                    nc.vector.tensor_tensor(at, at, strip[:, :, j, :], ALU.add)
                    last = dve.drain()
                last.then_inc(self.added, 1)

        staged = halves(piece(9))
        gcn_w = halves(piece(10))
        gcn_b = piece(11)[:, 0:D]
        FULL_CHUNKS = CHUNKS - 1

        stray_path(0)
        l1 = Agg(0)
        s_gw = sem("gcn1_weights_loaded")
        s_st = sem("chunk_staged1")
        s_gm = sem("chunk_projected1")
        s_t1 = sem("chunk_biased1")
        s_z2 = sem("z2_ready")
        s_z2s = sem("z2_stored")
        s_z2t = sem("z2_transposed")
        s_z2c = sem("z2_in_aggT")
        h_pre = halves(piece(0))
        z2 = halves(piece(1))

        def over_l1(eng, iteration):
            iteration(0, 0)
            iteration(1, 1)
            with eng.Fori(2, KV_ITERS - 1) as it:
                iteration(it, 2)
            iteration(KV_ITERS - 1, KV_ITERS - 1)
            iteration(KV_ITERS, KV_ITERS)
            with eng.Fori(Q_IT, Q_END) as it:
                iteration(it, Q_IT)
            for it in range(Q_END, ITERS):
                iteration(it, it)

        with nc.Block() as block:
            @block.gpsimd
            def _(pool):
                l1.pool_all(pool)

            @block.sync
            def _(sp):
                sp.dma_start(gcn_w, A["L0_gnn_W1"].rearrange("(k p) n -> p k n", p=P)).then_inc(s_gw, 16)
                sp.dma_start(gcn_b, row_bc(A["L0_gnn_b1"])).then_inc(s_gw, 16)

                def load_x(n, slot, uses):
                    c0, m, nj = q_rows(n)
                    rows_dram = x_tiles[bass.ds(c0, m * nj), :]
                    sp.dma_start(x_again[slot][0:m, 0:nj, :], rows_dram.rearrange("(j p) d -> p j d", p=m))\
                      .then_inc(s_rx[slot], 16)

                def store_residual(n, slot, uses):
                    c0, m, nj = q_rows(n)
                    sp.wait_ge(s_r, n + 1)
                    rows_dram = res_dram[bass.ds(c0, m * nj), :]
                    sp.dma_start(rows_dram.rearrange("(j p) d -> p j d", p=m), res_out[slot][0:m, 0:nj, :])\
                      .then_inc(s_rs[slot], 16)

                def store_z2(c):
                    sp.wait_ge(s_z2, c + 1)
                    sp.dma_start(z_dram[1][bass.ds(c * CH, CH), :].rearrange("(j p) d -> p j d", p=P), z2)\
                      .then_inc(s_z2s, 16)
                load_x(0, 0, 0)
                load_x(1, 1, 0)
                sp.sem_inc(s_rs[1], 16)
                with sp.Fori(0, Q_IT - 1) as c:
                    store_z2(c)
                store_residual(0, 0, 0)
                load_x(2, 0, 1)
                with sp.Fori(0, Q_END - Q_IT - 1) as i:
                    store_z2(Q_IT - 1 + i)
                    store_residual(2 * i + 1, 1, i)
                    load_x(2 * i + 3, 1, i + 1)
                    store_residual(2 * i + 2, 0, i + 1)
                    load_x(2 * i + 4, 0, i + 2)
                store_z2(Q_END - 2)
                store_residual(CHUNKS - 2, 1, None)
                store_residual(CHUNKS - 1, 0, None)
                for c in range(Q_END - 1, FULL_CHUNKS):
                    store_z2(c)
                sp.wait_ge(s_z2, CHUNKS)
                sp.dma_start(z_dram[1][FULL_CHUNKS * CH:N, :], z2[0:LAST, 0, :]).then_inc(s_z2s, 16)
                sp.wait_ge(s_z2s, 16 * CHUNKS)
                for slot in range(2):
                    sp.wait_ge(s_rs[slot], 16 * (CHUNKS // 2 + 1))

            @block.tensor
            def _(pe):
                t = nc.tensor
                pe.wait_ge(s_gw, 32)
                pe.wait_ge(s_w, 16 * 8)

                def post(c, nj, m):
                    pe.wait_ge(s_st, c + 1)
                    ge(pe, s_t1, c)
                    for j in range(nj):
                        for h in range(KH):
                            mm = t.matmul(ps[:, 6, j * 256:(j + 1) * 256], staged[:, h, j * P:(j + 1) * P],
                                          gcn_w[:, h, :], start=(h == 0), stop=(h == KH - 1))
                    mm.then_inc(s_gm, 1)
                    pe.wait_ge(s_z2, c + 1)
                    ge(pe, s_z2c, c)
                    for j in range(nj):
                        for h in range(KH):
                            mm = t.transpose(ps[:, 7, h * 256 + j * P:h * 256 + j * P + m],
                                             z2[0:m, j, h * P:(h + 1) * P], ident[0:m, 0:m])
                    mm.then_inc(s_z2t, 1)

                def iteration(it, lo):
                    for k in range(GI):
                        l1.pe(pe, it, k)
                        for work in mix_work(it, lo, k):
                            mix_pe(pe, *work)
                        l1.pe_turn(pe, it, k)
                        if k == PRE_STEP and lo > 0:
                            post(it - 1, 2, P)
                over_l1(pe, iteration)
                for k in range(G_REST):
                    l1.pe(pe, ITERS, k)
                    l1.pe_turn(pe, ITERS, k)
                    if k == PRE_STEP:
                        post(ITERS - 1, 2, P)
                post(ITERS, 1, LAST)

            @block.scalar
            def _(act):
                def post(c, nj, m):
                    act.wait_ge(s_t1, c + 1)
                    ge(act, s_z2s, 16 * c)
                    ge(act, s_z2t, c)
                    for j in range(nj):
                        a = nc.scalar.activation(z2[0:m, j, :], h_pre[0:m, j, :], ACT.Relu,
                                                 scale=dinv[0:m, bass.ds(2 * c + j, 1)])
                    a.then_inc(s_z2, 1)
                l1.act_first()

                mix_act_tile(0)

                def iteration(it, lo):
                    for k in range(GI):
                        l1.act(act, it, k)
                        for work in mix_work(it, lo, k):
                            mix_act(act, *work)
                        if k == PRE_STEP and lo > 0:
                            post(it - 1, 2, P)
                over_l1(act, iteration)
                for k in range(G_REST):
                    l1.act(act, ITERS, k)
                    if k == PRE_STEP:
                        post(ITERS - 1, 2, P)
                post(ITERS, 1, LAST)

            @block.vector
            def _(dve):
                v = nc.vector
                dve.wait_ge(s_gw, 32)
                dve.wait_ge(s_w, 16 * 8)
                dve.wait_ge(s_bd, 2 + P // DEPTH)

                def post(c, nj, m):
                    ge(dve, s_gm, c)
                    v.tensor_scalar(staged[:, :, 0:nj * P], aggT[:, :, bass.ds(c * CH, nj * P)], 1.0, None, ALU.mult)
                    dve.drain().then_inc(s_st, 1)
                    dve.wait_ge(s_gm, c + 1)
                    ge(dve, s_z2, c)
                    for j in range(nj):
                        v.scalar_tensor_tensor(h_pre[:, j, :], ps[:, 6, j * 256:(j + 1) * 256],
                                               dinv[:, bass.ds(2 * c + j, 1)], gcn_b, ALU.mult, ALU.add)
                    dve.drain().then_inc(s_t1, 1)
                    dve.wait_ge(s_z2t, c + 1)
                    n = (nj - 1) * P + m
                    v.tensor_scalar(aggT[:, :, bass.ds(c * CH, n)], halves(ps[:, 7, :])[:, :, 0:n], 1.0, None, ALU.mult)
                    dve.drain().then_inc(s_z2c, 1)

                l1.make_s(dve, 0, 0)

                def iteration(it, lo):
                    for k in range(GI):
                        l1.make_s(dve, it, k + 1)
                        for work in mix_work(it, lo, k):
                            mix_dve_first(dve, *work)
                        l1.add(dve, it, k)
                        for work in mix_work(it, lo, k):
                            mix_dve_second(dve, *work)
                        if k == PRE_STEP and lo > 0:
                            post(it - 1, 2, P)
                over_l1(dve, iteration)
                for k in range(G_REST):
                    if k < G_REST - 1:
                        l1.make_s(dve, ITERS, k + 1)
                    l1.add(dve, ITERS, k)
                    if k == PRE_STEP:
                        post(ITERS - 1, 2, P)
                post(ITERS, 1, LAST)

        w1 = big[:, 0:KH * NE * H].rearrange("p (k e h) -> p k e h", k=KH, e=NE)
        w2 = big[:, KH * NE * H:].rearrange("p (e c o) -> p e c o", e=NE, c=HC)
        hT = [scratch[:, 2 * b:2 * b + 2, :].rearrange("p a b -> p (a b)").rearrange("p (c n) -> p c n", c=HC)
              for b in range(2)]
        res_in = halves(piece(4))
        x2 = halves(piece(5))
        xn = halves(piece(6))
        xnT = halves(piece(7))
        y_acc = halves(piece(8))
        y_out = halves(piece(12))
        b2_sb = piece(11)[0:NE, D:2 * D]
        wT = piece(13)[0:NE, 0:CH]
        cmp = piece(13)[:, 256:256 + 128].rearrange("p (j e f) -> p j e f", j=2, e=NE)
        sm = lambda a, n: small[:, a:a + n]
        b1_col = sm(0, NE * HC)
        gam_col, bet_col = sm(32, 2), sm(34, 2)
        wr = sm(36, 16).rearrange("p (k e) -> p k e", k=KH)
        br_bc = sm(52, NE)
        st2 = sm(60, 12).rearrange("p (j c) -> p j c", j=2)
        mv2 = sm(72, 4).rearrange("p (j c) -> p j c", j=2)
        rs2 = sm(76, 2)
        var2 = sm(164, 2)
        logit = sm(78, 16).rearrange("p (j e) -> p j e", j=2)
        rank = sm(94, 16).rearrange("p (j e) -> p j e", j=2)
        top = sm(110, 16).rearrange("p (j e) -> p j e", j=2)
        gap = sm(126, 2)
        w_top = sm(128, 4).rearrange("p (a j) -> p a j", a=2)
        w_full = sm(132, 16).rearrange("p (j e) -> p j e", j=2)
        w_tmp = sm(148, 16).rearrange("p (j e) -> p j e", j=2)
        cmp2 = piece(13)[:, 384:384 + 128].rearrange("p (j e f) -> p j e f", j=2, e=NE)

        s_fw = sem("ffn_constants_loaded")
        with nc.Block() as block:
            @block.sync
            def _(sp):
                for h in range(KH):
                    sp.dma_start(w1[:, h, :, :], A["L0_ffn_W1"][:, h * P:(h + 1) * P, :].rearrange("e p h -> p e h"))\
                      .then_inc(s_fw, 16)
                sp.dma_start(w2.rearrange("p e c o -> p (e c) o"),
                             A["L0_ffn_W2"].rearrange("e (c p) o -> p (e c) o", p=P)).then_inc(s_fw, 16)
                sp.dma_start(gcn_w, A["L0_gnn_W2"].rearrange("(k p) n -> p k n", p=P)).then_inc(s_fw, 16)
                sp.dma_start(gcn_b, row_bc(A["L0_gnn_b2"])).then_inc(s_fw, 16)
                sp.dma_start(b2_sb, A["L0_ffn_b2"]).then_inc(s_fw, 16)
                sp.dma_start(wr, A["L0_ffn_Wr"].rearrange("(k p) e -> p k e", p=P)).then_inc(s_fw, 16)
                sp.dma_start(br_bc, row_bc(A["L0_ffn_br"])).then_inc(s_fw, 16)
                with nc.allow_non_contiguous_dma(reason="vectors with one element per partition"):
                    sp.dma_start(b1_col, A["L0_ffn_b1"].rearrange("e (c p) -> p (e c)", p=P)).then_inc(s_fw, 16)
                    sp.dma_start(gam_col, A["L0_ffn_gamma"].rearrange("(k p) -> p k", p=P)).then_inc(s_fw, 16)
                    sp.dma_start(bet_col, A["L0_ffn_beta"].rearrange("(k p) -> p k", p=P)).then_inc(s_fw, 16)
                sp.wait_ge(s_fw, 16 * 11)

        stray_path(1)
        l2 = Agg(1)
        s_rl = sem("residual_loaded")
        s_st = sem("chunk_staged2")
        s_gm = sem("chunk_projected2")
        s_x2 = sem("x2_ready")
        s_xn = sem("xn_ready")
        s_xnp = sem("xn_transposed")
        s_xnt = sem("xnT_ready")
        s_lg = sem("logits_done")
        s_gap = sem("top_gap_ready")
        s_th = sem("top_tanh_ready")
        s_wf = sem("expert_weights_ready")
        s_wt = sem("expert_weights_transposed")
        s_wc = sem("expert_weights_T_ready")
        s_yb = sem("expert_bias_done")
        s_yb_read = sem("expert_bias_read")
        s_hd = sem("hidden_projected")
        s_ge = sem("gelu_done")
        s_yd = sem("expert_projected")
        s_ya = sem("expert_added")
        s_yo = sem("chunk_out_ready")
        s_ys = sem("chunk_stored")

        class Chunk:

            def __init__(self, c):
                self.c = c
                whole = not isinstance(c, int) or c < FULL_CHUNKS
                self.nj = 2 if whole else 1
                self.m = P if whole else LAST
                self.n = self.nj * P

        with nc.Block() as block:
            @block.gpsimd
            def _(pool):
                l2.pool_all(pool)

            def over_iterations(eng, step):
                for k in range(GI):
                    step(0, k, True, None, None)
                for k in range(GI):
                    step(1, k, True, None, Chunk(0))
                for k in range(GI):
                    step(2, k, True, Chunk(0), Chunk(1))
                with eng.Fori(3, ITERS) as it:
                    for k in range(GI):
                        step(it, k, True, Chunk(it - 2), Chunk(it - 1))
                for k in range(GI):
                    step(ITERS, k, k < G_REST, Chunk(ITERS - 2), Chunk(ITERS - 1))
                for k in range(GI):
                    step(ITERS + 1, k, False, Chunk(ITERS - 1), Chunk(ITERS))
                for k in range(4):
                    step(ITERS + 2, k, False, Chunk(ITERS), None)

            @block.sync
            def _(sp):
                def load(c, nj, m):
                    ge(sp, s_x2, c)
                    if nj == 2:
                        sp.dma_start(res_in, res_dram[bass.ds(c * CH, CH), :].rearrange("(j p) d -> p j d", p=P))\
                          .then_inc(s_rl, 16)
                    else:
                        sp.dma_start(res_in[0:m, 0, :], res_dram[c * CH:N, :]).then_inc(s_rl, 16)

                def store(c, nj, m):
                    sp.wait_ge(s_yo, c + 1)
                    if nj == 2:
                        sp.dma_start(out[bass.ds(c * CH, CH), :].rearrange("(j p) d -> p j d", p=P), y_out)\
                          .then_inc(s_ys, 16)
                    else:
                        sp.dma_start(out[c * CH:N, :], y_out[0:m, 0, :]).then_inc(s_ys, 16)
                load(0, 2, P)
                load(1, 2, P)
                with sp.Fori(0, FULL_CHUNKS - 2) as c:
                    store(c, 2, P)
                    load(c + 2, 2, P)
                store(FULL_CHUNKS - 2, 2, P)
                load(FULL_CHUNKS, 1, LAST)
                store(FULL_CHUNKS - 1, 2, P)
                store(FULL_CHUNKS, 1, LAST)
                sp.wait_ge(s_ys, 16 * CHUNKS)

            @block.tensor
            def _(pe):
                t = nc.tensor

                def up(ch, e):
                    x = NE * ch.c + e
                    for c in range(HC):
                        if c % 2 == 0:
                            ge(pe, s_ge, 2 * x - 1 + c // 2)
                        for h in range(KH):
                            mm = t.matmul(ps[:, 2 + c // 2, (c % 2) * 256:(c % 2) * 256 + ch.n],
                                          w1[:, h, e, c * P:(c + 1) * P], xnT[:, h, 0:ch.n],
                                          start=(h == 0), stop=(h == KH - 1))
                        if c % 2:
                            mm.then_inc(s_hd, 1)

                def down(ch, e, tiles=range(2)):
                    x = NE * ch.c + e
                    b = e % 2
                    if tiles[0] == 0:
                        pe.wait_ge(s_ge, 2 * x + 2)
                        ge(pe, s_ya, x - 1)
                    for j in tiles:
                        if j < ch.nj:
                            for c in range(HC):
                                mm = t.matmul(ps[:, 4 + b, j * 256:(j + 1) * 256], hT[b][:, c, j * P:(j + 1) * P],
                                              w2[:, e, c, :], start=(c == 0), stop=(c == HC - 1))
                            if j == ch.nj - 1:
                                mm.then_inc(s_yd, 1)

                def expert(ch, e):
                    up(ch, e)
                    down(ch, e - 1)

                def gcn(ch):
                    pe.wait_ge(s_st, ch.c + 1)
                    ge(pe, s_yb_read, ch.c)
                    for j in range(ch.nj):
                        for h in range(KH):
                            mm = t.matmul(ps[:, 6, j * 256:(j + 1) * 256], staged[:, h, j * P:(j + 1) * P],
                                          gcn_w[:, h, :], start=(h == 0), stop=(h == KH - 1))
                    mm.then_inc(s_gm, 1)

                def transpose_xn(ch):
                    pe.wait_ge(s_xn, ch.c + 1)
                    ge(pe, s_wc, ch.c)
                    for j in range(ch.nj):
                        for h in range(KH):
                            mm = t.transpose(ps[:, 7, h * 256 + j * P:h * 256 + (j + 1) * P],
                                             xn[:, j, h * P:(h + 1) * P], ident[:, :])
                    mm.then_inc(s_xnp, 1)

                def logits(ch):
                    pe.wait_ge(s_xnt, ch.c + 1)
                    for j in range(ch.nj):
                        for h in range(KH):
                            mm = t.matmul(ps[:, 6, j * NE:(j + 1) * NE], xnT[:, h, j * P:(j + 1) * P], wr[:, h, :],
                                          start=(h == 0), stop=(h == KH - 1))
                    mm.then_inc(s_lg, 1)

                def turn_weights(ch):
                    pe.wait_ge(s_wf, ch.c + 1)
                    for j in range(ch.nj):
                        mm = t.transpose(ps[0:NE, 7, j * P:(j + 1) * P], w_full[:, j, :], ident[:, :])
                    mm.then_inc(s_wt, 1)

                def bias(ch):
                    pe.wait_ge(s_wc, ch.c + 1)
                    for j in range(ch.nj):
                        mm = t.matmul(ps[:, 6, j * 256:(j + 1) * 256], wT[:, j * P:(j + 1) * P], b2_sb,
                                      start=True, stop=True)
                    mm.then_inc(s_yb, 1)

                def step(it, k, agg, prev, cur):
                    if agg:
                        l2.pe(pe, it, k)
                    if prev and k <= 2:
                        expert(prev, (4, 5, 7)[k])
                    if k == 3:
                        if prev:
                            down(prev, 7, [0])
                        if cur:
                            transpose_xn(cur)
                        if prev:
                            down(prev, 7, [1])
                    if cur and k >= 4:
                        expert(cur, k - 2)
                    if agg:
                        l2.pe_turn(pe, it, k)
                    if k == PRE_STEP:
                        if prev:
                            expert(prev, 6)
                        if cur:
                            gcn(cur)
                    if k == 3 and cur:
                        logits(cur)
                        up(cur, 0)
                        up(cur, 1)
                        turn_weights(cur)
                        down(cur, 0)
                        bias(cur)
                over_iterations(pe, step)

            @block.scalar
            def _(act):
                a = nc.scalar

                def gelu(ch, e):
                    x = NE * ch.c + e
                    ge(act, s_yd, x - 1)
                    for c in range(HC):
                        if c % 2 == 0:
                            act.wait_ge(s_hd, 2 * x + c // 2 + 1)
                        last = a.activation(hT[e % 2][:, c, 0:ch.n], ps[:, 2 + c // 2, (c % 2) * 256:(c % 2) * 256 + ch.n],
                                            ACT.Gelu, bias=b1_col[:, e * HC + c:e * HC + c + 1])
                        if c % 2:
                            last.then_inc(s_ge, 1)

                def evac_xn(ch):
                    act.wait_ge(s_xnp, ch.c + 1)
                    for h in range(KH):
                        last = a.activation(xnT[:, h, 0:ch.n], ps[:, 7, h * 256:h * 256 + ch.n], ACT.Identity,
                                            bias=bet_col[:, h:h + 1], scale=gam_col[:, h:h + 1])
                    last.then_inc(s_xnt, 1)

                def softmax(ch):
                    act.wait_ge(s_gap, ch.c + 1)
                    a.activation(gap[:, :], gap[:, :], ACT.Tanh, scale=0.5).then_inc(s_th, 1)

                l2.act_first()

                def step(it, k, agg, prev, cur):
                    if agg:
                        l2.act(act, it, k)
                    if k <= 2 and prev:
                        for e in ((4,), (5, 6), (7,))[k]:
                            gelu(prev, e)
                    if k == 3 and cur:
                        evac_xn(cur)
                        softmax(cur)
                        gelu(cur, 0)
                        gelu(cur, 1)
                    if k >= 4 and cur:
                        gelu(cur, k - 2)
                over_iterations(act, step)

            @block.vector
            def _(dve):
                v = nc.vector

                def finish_gcn(ch):
                    c, nj = ch.c, ch.nj
                    dve.wait_ge(s_gm, c + 1)
                    for j in range(nj):
                        v.scalar_tensor_tensor(x2[:, j, :], ps[:, 6, j * 256:(j + 1) * 256],
                                               dinv[:, bass.ds(2 * c + j, 1)], gcn_b, ALU.mult, ALU.add)
                    dve.drain()
                    dve.wait_ge(s_rl, 16 * (c + 1))
                    v.scalar_tensor_tensor(x2[:, 0:nj, :], x2[:, 0:nj, :], 0.0, res_in[:, 0:nj, :], ALU.max, ALU.add)
                    dve.drain().then_inc(s_x2, 1)
                    ge(dve, s_xnp, c)
                    src = x2
                    for _ in range(2):
                        for j in range(nj):
                            v.bn_stats(st2[:, j, :], src[:, j, :])
                        dve.drain()
                        for j in range(nj):
                            v.bn_aggr(mv2[:, j, :], st2[:, j, :])
                        dve.drain()
                        v.tensor_scalar(var2[:, 0:nj], mv2[:, 0:nj, 1], EPS, None, ALU.add)
                        dve.drain()
                        rsqrt(dve, rs2[:, 0:nj], var2[:, 0:nj], sm(166, nj))
                        for j in range(nj):
                            v.tensor_scalar(xn[:, j, :], src[:, j, :], mv2[:, j, 0:1], rs2[:, j:j + 1],
                                            ALU.subtract, ALU.mult)
                        dve.drain()
                        src = xn
                    v.nop().then_inc(s_xn, 1)

                def stage(ch):
                    v.tensor_copy(staged[:, :, 0:ch.n], aggT[:, :, bass.ds(ch.c * CH, ch.n)])
                    dve.drain().then_inc(s_st, 1)

                def add_expert(ch, e):
                    x = NE * ch.c + e
                    dve.wait_ge(s_yd, x + 1)
                    dst = y_acc if e < NE - 1 else y_out
                    if e == NE - 1:
                        ge(dve, s_ys, 16 * ch.c)
                    for j in range(ch.nj):
                        v.scalar_tensor_tensor(dst[:, j, :], ps[:, 4 + e % 2, j * 256:(j + 1) * 256],
                                               w_full[:, j, e:e + 1], y_acc[:, j, :], ALU.mult, ALU.add)
                    dve.drain().then_inc(s_ya, 1)
                    if e == NE - 1:
                        v.nop().then_inc(s_yo, 1)

                def route(ch):
                    c, nj = ch.c, ch.nj
                    dve.wait_ge(s_lg, c + 1)
                    L = logit[:, 0:nj, :]
                    v.tensor_tensor(L, ps[:, 6, 0:nj * NE].rearrange("p (j e) -> p j e", e=NE),
                                    br_bc.unsqueeze(1).to_broadcast([P, nj, NE]), ALU.add)
                    dve.drain()
                    for j in range(nj):
                        v.max(out=top[:, j, :], in_=logit[:, j, :])
                        mine = logit[:, j, :].unsqueeze(2).to_broadcast([P, NE, NE])
                        theirs = logit[:, j, :].unsqueeze(1).to_broadcast([P, NE, NE])
                        v.tensor_tensor(cmp[:, j, :, :], theirs, mine, ALU.is_gt)
                        v.tensor_tensor(cmp2[:, j, :, :], theirs, mine, ALU.is_equal)
                    dve.drain()
                    for j in range(nj):
                        v.tensor_tensor(cmp2[:, j, :, :], cmp2[:, j, :, :], before[:, :, :], ALU.mult)
                    v.tensor_tensor(gap[:, 0:nj], top[:, 0:nj, 0], top[:, 0:nj, 1], ALU.subtract)
                    if nj == 1:
                        v.memset(gap[:, 1:2], 0.0)
                    dve.drain().then_inc(s_gap, 1)
                    v.tensor_tensor(cmp[:, 0:nj, :, :].rearrange("p j e f -> p (j e f)"),
                                    cmp[:, 0:nj, :, :].rearrange("p j e f -> p (j e f)"),
                                    cmp2[:, 0:nj, :, :].rearrange("p j e f -> p (j e f)"), ALU.add)
                    dve.drain()
                    v.reduce_sum(rank[:, 0:nj, :].rearrange("p j e -> p (j e)"),
                                 cmp[:, 0:nj, :, :].rearrange("p j e f -> p (j e) f"), axis=AX_X)
                    dve.wait_ge(s_th, c + 1)
                    v.tensor_scalar(w_top[:, 0, :], gap[:, :], 0.5, 0.5, ALU.mult, ALU.add)
                    v.tensor_scalar(w_top[:, 1, :], gap[:, :], -0.5, 0.5, ALU.mult, ALU.add)
                    dve.drain()
                    for j in range(nj):
                        v.tensor_scalar(w_tmp[:, j, :], rank[:, j, :], 0.0, w_top[:, 0, j:j + 1],
                                        ALU.is_equal, ALU.mult)
                        v.tensor_scalar(w_full[:, j, :], rank[:, j, :], 1.0, w_top[:, 1, j:j + 1],
                                        ALU.is_equal, ALU.mult)
                    dve.drain()
                    v.tensor_tensor(w_full[:, 0:nj, :], w_full[:, 0:nj, :], w_tmp[:, 0:nj, :], ALU.add)
                    dve.drain().then_inc(s_wf, 1)

                def start_y(ch):
                    c, nj = ch.c, ch.nj
                    dve.wait_ge(s_wt, c + 1)
                    v.tensor_copy(wT[:, 0:ch.n], ps[0:NE, 7, 0:ch.n]).then_inc(s_wc, 1)
                    dve.wait_ge(s_yb, c + 1)
                    v.tensor_tensor(y_acc[:, 0:nj, :], x2[:, 0:nj, :], halves(ps[:, 6, :])[:, 0:nj, :], ALU.add)
                    dve.drain().then_inc(s_yb_read, 1)

                def step(it, k, agg, prev, cur):
                    if agg and not (isinstance(it, int) and GI * it + k == GROUPS - 1):
                        l2.make_s(dve, it, k + 1)
                    if prev and k <= 3:
                        add_expert(prev, (3, 4, 6, 7)[k])
                    if cur and k >= 4:
                        add_expert(cur, k - 3)
                    if cur and k == 3:
                        route(cur)
                    if agg:
                        l2.add(dve, it, k)
                    if k == PRE_STEP:
                        if cur:
                            stage(cur)
                        if prev:
                            add_expert(prev, 5)
                        if cur:
                            finish_gcn(cur)
                    if k == 3 and cur:
                        start_y(cur)
                        add_expert(cur, 0)
                l2.make_s(dve, 0, 0)
                over_iterations(dve, step)


_INS = ["x", "src", "dst", "edge_weight", "L0_gnn_W1", "L0_gnn_b1", "L0_gnn_W2", "L0_gnn_b2",
        "L0_mix_wq", "L0_mix_bq", "L0_mix_wk", "L0_mix_bk", "L0_mix_wv", "L0_mix_bv", "L0_mix_wo", "L0_mix_bo",
        "L0_ffn_gamma", "L0_ffn_beta", "L0_ffn_Wr", "L0_ffn_br", "L0_ffn_W1", "L0_ffn_b1", "L0_ffn_W2", "L0_ffn_b2"]


def kernel(**inputs):
    import numpy as _np
    import concourse.bacc as _bacc
    from concourse import mybir as _mybir
    from concourse.bass_utils import run_bass_kernel_spmd as _run

    nc = _bacc.Bacc("TRN2", target_bir_lowering=False, num_devices=1)
    arrays, aps = {}, {}
    for name in _INS:
        a = _np.ascontiguousarray(inputs[name])
        arrays[f"in_{name}"] = a
        aps[name] = nc.dram_tensor(f"in_{name}", a.shape, _mybir.dt.from_np(a.dtype), kind="ExternalInput").ap()
    out = nc.dram_tensor("out_0", (N, D), F32, kind="ExternalOutput").ap()
    gps_layer(nc, aps, out)
    r = _run(nc, [arrays], core_ids=[0])
    return r.results[0]["out_0"]
```
